# Optimizing a Trainium2 kernel written in Bass

```python
import numpy as np
import jax
import jax.numpy as jnp

def _softmax(x, axis=-1):
    return jax.nn.softmax(x, axis=axis)

def _gelu(x):
    return jax.nn.gelu(x, approximate=True)

def _silu(x):
    return jax.nn.silu(x)

def _sigmoid(x):
    return jax.nn.sigmoid(x)

def _layernorm(x, axis=-1, eps=1e-05):
    m = jnp.mean(x, axis=axis, keepdims=True)
    v = jnp.var(x, axis=axis, keepdims=True)
    return (x - m) / jnp.sqrt(v + eps)

def _scatter_add(tgt, idx, src, axis=0):
    return tgt.at[idx].add(src)

def _segment_sum(src, seg, n):
    return jax.ops.segment_sum(src, seg, n)
kernel_name = 'mk_flamingo_gated_d1_seqx_r8_5d5a45'

def setup_inputs(seed: int=0):
    np.random.seed(seed)
    _w = jnp.asarray

    def _rec_inputs():
        import jax
        import jax.numpy as jnp
        _rk = jax.random.key(seed)
        x = -0.0002928 + 1 * jax.random.normal(jax.random.fold_in(_rk, 1), (4, 256, 256), jnp.float32)
        _lenS = 256 - jax.random.randint(jax.random.fold_in(_rk, 7), (4,), 0, max(1, 256 // 4) + 1, jnp.int32)
        _lenS2 = 256 - jax.random.randint(jax.random.fold_in(_rk, 8), (4,), 0, max(1, 256 // 4) + 1, jnp.int32)
        _ctx_512P = jax.random.normal(jax.random.fold_in(_rk, 11), (4, 16, 64), jnp.float32)
        _ctx_512c = jax.random.dirichlet(jax.random.fold_in(_rk, 511), 0.3 * jnp.ones((16,), jnp.float32), (4, 256))
        _ctx_512t = jnp.einsum('bsk,bkd->bsd', _ctx_512c, _ctx_512P)
        _ctx_512t = _ctx_512t * jax.lax.rsqrt(jnp.mean(jnp.square(_ctx_512t)) + 1e-12) * 0.953939
        ctx_512 = 0.000227908 + 0.99994 * (_ctx_512t + 0.3 * jax.random.normal(jax.random.fold_in(_rk, 611), (4, 256, 64), jnp.float32))
        _g = jax.random.normal(jax.random.fold_in(_rk, 9001), (2, 1), jnp.float32)
        _g = jnp.sign(_g) * jnp.maximum(jnp.abs(_g), 1.0) + (_g == 0) * 1.0
        g_xattn = _g[0]
        g_ffn = _g[1]
        return (x, ctx_512, g_xattn, g_ffn)
    x, ctx_512, g_xattn, g_ffn = _rec_inputs()

    def _L0_xattn_setup():
        import jax, jax.numpy as jnp
        import numpy as np
        B, S, L = (2, 128, 128)
        DIM_Q, H, K, D_C, D_CQ, R = (256, 16, 128, 64, 192, 64)

        def _rope_tables(seq_len, dim, dtype):
            inv_freq = 1.0 / 10000.0 ** (jnp.arange(0, dim, 2, dtype=dtype) / dim)
            t = jnp.arange(seq_len, dtype=dtype)
            freqs = t[:, None] * inv_freq[None, :]
            sin = jnp.repeat(jnp.sin(freqs), 2, axis=-1)
            cos = jnp.repeat(jnp.cos(freqs), 2, axis=-1)
            return (sin, cos)

        def _rotate_half(x):
            h = x.shape[-1] // 2
            return jnp.concatenate([-x[..., h:], x[..., :h]], axis=-1)
        key = jax.random.key(seed)
        ks = jax.random.split(key, 8)
        s_in = 1.0 / np.sqrt(DIM_Q)
        s_k = 1.0 / np.sqrt(K)
        s_cq = 1.0 / np.sqrt(D_CQ)
        s_c = 1.0 / np.sqrt(D_C)
        return {'hidden_q': jax.random.normal(ks[0], (B, S, DIM_Q), jnp.float32), 'kv_c': jax.random.normal(ks[1], (B, L, D_C), jnp.float32), 'Wq': jax.random.normal(ks[2], (H * K, DIM_Q), jnp.float32) * s_in, 'w_kc_q': jax.random.normal(ks[3], (H, K, D_CQ), jnp.float32) * s_k, 'w_kc_kv': jax.random.normal(ks[4], (H, K, D_C), jnp.float32) * s_k, 'W_qr': jax.random.normal(ks[5], (H, D_CQ, R), jnp.float32) * s_cq / np.sqrt(R), 'W_kr': jax.random.normal(ks[6], (H, D_C, R), jnp.float32) * s_c, 'Wo': jax.random.normal(ks[7], (DIM_Q, H * K), jnp.float32) * s_k}
    _L0_xattn_all = _L0_xattn_setup()
    _L0_xattn_in = {k: v for k, v in _L0_xattn_all.items() if k in ('Wq', 'w_kc_q', 'w_kc_kv', 'W_qr', 'W_kr', 'Wo')}
    del _L0_xattn_all

    def _L0_ffn_setup():
        import jax, jax.numpy as jnp
        import numpy as np
        key = jax.random.key(seed)
        k1, k2, k3, k4 = jax.random.split(key, 4)
        B, S, D_IN, D_OUT = (4, 512, 256, 256)
        x = jax.random.normal(k1, (B, S, D_IN), dtype=jnp.float32)
        weight = jax.random.normal(k2, (D_OUT, D_IN), dtype=jnp.float32) * 0.02
        scale_weight = jax.random.uniform(k3, (D_OUT,), dtype=jnp.float32, minval=0.5, maxval=1.5)
        bias = jax.random.normal(k4, (D_OUT,), dtype=jnp.float32) * 0.02
        return {'x': x, 'weight': weight, 'scale_weight': scale_weight, 'bias': bias}
    _L0_ffn_all = _L0_ffn_setup()
    _L0_ffn_in = {k: v for k, v in _L0_ffn_all.items() if k in ('weight', 'scale_weight', 'bias')}
    del _L0_ffn_all
    return {'x': x, 'ctx_512': ctx_512, 'g_xattn': g_xattn, 'g_ffn': g_ffn, 'L0_xattn_Wq': _L0_xattn_in['Wq'], 'L0_xattn_w_kc_q': _L0_xattn_in['w_kc_q'], 'L0_xattn_w_kc_kv': _L0_xattn_in['w_kc_kv'], 'L0_xattn_W_qr': _L0_xattn_in['W_qr'], 'L0_xattn_W_kr': _L0_xattn_in['W_kr'], 'L0_xattn_Wo': _L0_xattn_in['Wo'], 'L0_ffn_weight': _L0_ffn_in['weight'], 'L0_ffn_scale_weight': _L0_ffn_in['scale_weight'], 'L0_ffn_bias': _L0_ffn_in['bias']}

def reference(x, ctx_512, g_xattn, g_ffn, L0_xattn_Wq, L0_xattn_w_kc_q, L0_xattn_w_kc_kv, L0_xattn_W_qr, L0_xattn_W_kr, L0_xattn_Wo, L0_ffn_weight, L0_ffn_scale_weight, L0_ffn_bias):
    import jax
    import jax.numpy as jnp

    def _L0_xattn_ref(hidden_q, kv_c, Wq, w_kc_q, w_kc_kv, W_qr, W_kr, Wo):
        import jax, jax.numpy as jnp
        import numpy as np
        B, S, L = (2, 128, 128)
        DIM_Q, H, K, D_C, D_CQ, R = (256, 16, 128, 64, 192, 64)

        def _rope_tables(seq_len, dim, dtype):
            inv_freq = 1.0 / 10000.0 ** (jnp.arange(0, dim, 2, dtype=dtype) / dim)
            t = jnp.arange(seq_len, dtype=dtype)
            freqs = t[:, None] * inv_freq[None, :]
            sin = jnp.repeat(jnp.sin(freqs), 2, axis=-1)
            cos = jnp.repeat(jnp.cos(freqs), 2, axis=-1)
            return (sin, cos)

        def _rotate_half(x):
            h = x.shape[-1] // 2
            return jnp.concatenate([-x[..., h:], x[..., :h]], axis=-1)
        b, s, _ = hidden_q.shape
        l = kv_c.shape[1]
        q_hk = (hidden_q @ Wq.T).reshape(b, s, H, K)
        q_big = jnp.einsum('bshk,hkq->bshq', q_hk, w_kc_q)
        sin, cos = _rope_tables(l, D_C, kv_c.dtype)
        kv_rope = kv_c * cos[None] + _rotate_half(kv_c) * sin[None]
        q_r = jnp.einsum('bshq,hqr->bhsr', q_big, W_qr)
        k_r = jnp.einsum('bld,hdr->bhlr', kv_rope, W_kr)
        scores = jnp.einsum('bhsr,bhlr->bhsl', q_r, k_r)
        attn = jax.nn.softmax(scores, axis=-1)
        ctx_c = jnp.einsum('bhsl,bld->bhsd', attn, kv_rope)
        ctx_lat = jnp.einsum('bhsd,hkd->bshk', ctx_c, w_kc_kv)
        out = ctx_lat.reshape(b, s, H * K) @ Wo.T
        return out

    def _L0_ffn_ref(x, weight, scale_weight, bias):
        import jax, jax.numpy as jnp
        import numpy as np
        w = weight * scale_weight[:, None]
        out = jnp.einsum('bsi,oi->bso', x, w) + bias
        return out
    x = x + jnp.tanh(g_xattn[0]) * _L0_xattn_ref(_layernorm(x, axis=-1), ctx_512, L0_xattn_Wq, L0_xattn_w_kc_q, L0_xattn_w_kc_kv, L0_xattn_W_qr, L0_xattn_W_kr, L0_xattn_Wo)
    x = x + jnp.tanh(g_ffn[0]) * _L0_ffn_ref(_layernorm(x, axis=-1), L0_ffn_weight, L0_ffn_scale_weight, L0_ffn_bias)
    return x

_drawn_inputs = setup_inputs


def setup_inputs(seed=0):
    import zlib

    import numpy as np

    out = dict(_drawn_inputs(seed))
    spreads = {}
    factors = {'L0_ffn_bias': 4.489}
    for name, (base, spread) in spreads.items():
        noise = np.random.default_rng([zlib.crc32(name.encode()), seed]).standard_normal(out[name].shape)
        drawn = base * np.exp(spread * noise) if base else spread * noise
        out[name] = jnp.asarray(drawn.astype(out[name].dtype))
    for name, factor in factors.items():
        out[name] = (out[name] * factor).astype(out[name].dtype)
    return out
```

```python
from contextlib import ExitStack

import concourse.bass as bass
from concourse import mybir

P = 128
F32 = mybir.dt.float32
F32R = mybir.dt.float32r
F16 = mybir.dt.float16
ACT = mybir.ActivationFunctionType
ALU = mybir.AluOpType
AX_X = mybir.AxisListType.X
RMAX = bass.bass_isa.ReduceOp.max

B, S, DM = 4, 256, 256
H, K, DC, DQ, R = 16, 128, 64, 192, 64
T = B * S
NT = T // P
NP = H // 2
STEPS = NP * B
IC = DM // P
SC = S // P
QC = 96
EPS = 1e-5
V_TOP = 1024.0
TINY = 1e-20


def flamingo_kernel(nc, x, kv_rows, kv_cols, rope_rows, rope_cols, identity, w_f1, w_q, w_kr, w_o,
                    w_ffn, rows_o, gates, out):
    ctx = ExitStack()
    with ctx:
        def sb(name, shape, dt=F32):
            return ctx.enter_context(nc.sbuf_tensor(name, shape, dt))

        def pb(name, shape):
            return ctx.enter_context(nc.psum_tensor(name, shape, F32))

        def sem(name):
            return ctx.enter_context(nc.semaphore(name))

        x_sb = sb("x_sb", [P, NT, DM])
        kvn = sb("kvn", [P, 2, NT * DC])
        kvt = sb("kvt", [P, 2, T])
        ropen = sb("ropen", [P, 2, SC * DC])
        ropet = sb("ropet", [P, 2, S])
        ident = sb("ident", [P, P])
        f1w = sb("f1w", [QC, 2 * 2 * K + 2 * 2 * R])
        wq = sb("wq", [P, 2, DM])
        wkr = sb("wkr", [P, P])
        wo = sb("wo", [P, 2 * DC + 2 * DM])
        ffn_raw = sb("ffn_raw", [P, IC, DM])
        rowo = sb("rowo", [P, 2, DM])
        gate = sb("gate", [P, 2])
        stats = sb("stats", [P, NT, 6])
        mv = sb("mv", [P, NT, 2])
        std = sb("std", [P, NT])
        rstd = sb("rstd", [P, NT])
        eps = sb("eps", [P, 1])
        xn = sb("xn", [P, NT, DM])
        xt_hi = sb("xt_hi", [P, IC, T], F32R)
        xt_lo = sb("xt_lo", [P, IC, T], F32R)
        kt = sb("kt", [P, T])
        kt2 = sb("kt2", [P, T])
        k_hi = sb("k_hi", [P, T], F32R)
        k_lo = sb("k_lo", [DC + 1, T], F32R)
        vn = sb("vn", [P, NT, DC])
        vn2 = sb("vn2", [P, NT, DC])
        v_hi = sb("v_hi", [P, NT, DC + 1], F16)
        v_lo = sb("v_lo", [P, NT, DC], F16)
        vmax = sb("vmax", [P, 1])
        vall = sb("vall", [P, 1])
        vinv = sb("vinv", [P, 1])
        vscale = sb("vscale", [P, 1])
        tanhs = sb("tanhs", [P, 2])
        ga = sb("ga", [P, 1])
        wffn = sb("wffn", [P, IC, DM])
        gbias = sb("gbias", [P, DM])
        g_sb = sb("g_sb", [P, P])
        mt_sb = sb("mt_sb", [P, DM])
        m_hi = sb("m_hi", [P, IC, P], F32R)
        m_lo = sb("m_lo", [P, IC, P], F32R)
        n_hi = sb("n_hi", [P, NP, DM], F32R)
        n_lo = sb("n_lo", [P, NP, DM], F32R)
        q_hl = sb("q_hl", [P, B, 2, S], F32R)
        q_hm = sb("q_hm", [DC + 1, B, 2, S], F32R)
        mx = sb("mx", [P, B, 4])
        mxt = sb("mxt", [4, B, P], F32R)
        p_f32 = sb("p_f32", [P, 2, 4 * S])
        p_hi = sb("p_hi", [P, B, SC, 2, S], F16)
        p_lo = sb("p_lo", [P, B, SC, 2, S], F16)
        rden = sb("rden", [P, B, 4])
        cx = sb("cx", [P, NT, NP, P])
        ct_hi = sb("ct_hi", [P, 2, NP, P], F32R)
        ct_lo = sb("ct_lo", [P, 2, NP, P], F32R)
        x1 = sb("x1", [P, 2, DM])
        x1b = sb("x1b", [P, 2, DM])
        xn2 = sb("xn2", [P, 2, DM])
        st2 = sb("st2", [P, 2, 6])
        mv2 = sb("mv2", [P, 2, 2])
        sd2 = sb("sd2", [P, 2])
        rs2 = sb("rs2", [P, 2])
        xt2 = sb("xt2", [P, 2, IC, P])
        y = sb("y", [P, 2, DM])

        ps_s = pb("ps_s", [P, 2, 512])
        ps_t = pb("ps_t", [P, 2, SC, 512])
        ps_c = pb("ps_c", [P, 512])
        ps_a = pb("ps_a", [P, 512])
        ps_f = ps_s[:, 1, :]

        def ps_o(t):
            return (ps_c if t % 2 else ps_a)[:, 0:DM]

        x_in = [sem(f"x_in{i}") for i in range(2)]
        kvn_in, kvt_in, rope_in, ident_in = sem("kvn_in"), sem("kvt_in"), sem("rope_in"), sem("ident_in")
        f1w_in, wq_in, wkr_in, wo_in = sem("f1w_in"), sem("wq_in"), sem("wkr_in"), sem("wo_in")
        ffn_in, small_in = sem("ffn_in"), sem("small_in")
        qhm_in = [sem(f"qhm_in{b}") for b in range(B)]
        mrow_in = [sem(f"mrow_in{b}") for b in range(B)]
        y_out = [sem(f"y_out{i}") for i in range(2)]
        xt_done, f1_done, f2_done, f3_done, nf_done = (sem(n) for n in (
            "xt_done", "f1_done", "f2_done", "f3_done", "nf_done"))
        q_done, s_done, st_done, mt_done, pv_done = (sem(n) for n in (
            "q_done", "s_done", "st_done", "mt_done", "pv_done"))
        ctt_done, o_done, xt2_done, ffn_done = (sem(n) for n in (
            "ctt_done", "o_done", "xt2_done", "ffn_done"))
        xthi_set, khi_set, g_set, mtsb_set, mhi_set, nhi_set = (sem(n) for n in (
            "xthi_set", "khi_set", "g_set", "mtsb_set", "mhi_set", "nhi_set"))
        qhi_set, p32_set, phi_set, mxt_set = (sem(n) for n in ("qhi_set", "p32_set", "phi_set", "mxt_set"))
        std_set, std2_set = sem("std_set"), sem("std2_set")
        tanh_set, cthi_set, xt2_set = sem("tanh_set"), sem("cthi_set"), sem("xt2_set")
        dve = sem("dve")
        xn_set, xtlo_set, klo_set, v_set, mlo_set, nlo_set = (sem(n) for n in (
            "xn_set", "xtlo_set", "klo_set", "v_set", "mlo_set", "nlo_set"))
        max_set, qlo_set, plo_set, cx_set = (sem(n) for n in ("max_set", "qlo_set", "plo_set", "cx_set"))
        vmax_set, const_set, ctlo_set, x1_set, xn2_set, y_set = (sem(n) for n in (
            "vmax_set", "const_set", "ctlo_set", "x1_set", "xn2_set", "y_set"))
        rec_set, var_set, var2_set = sem("rec_set"), sem("var_set"), sem("var2_set")
        pool = sem("pool")
        kt_set, vn_set, vall_set, x1b_set = sem("kt_set"), sem("vn_set"), sem("vall_set"), sem("x1b_set")

        def wait(eng, s, n):
            if not isinstance(n, int) or n > 0:
                eng.wait_ge(s, n)

        def pairs(eng, step):
            step(0)
            with eng.Fori(1, NP - 2) as p:
                step(p)
            step(NP - 2)
            step(NP - 1)

        def is_at_most(p, last):
            return p <= last if isinstance(p, int) else True

        block = ctx.enter_context(nc.Block())

        @block.sync
        def _(sp):
            def load(buf, src, landed):
                sp.dma_start(buf, src).then_inc(landed, 16)

            load(f1w[:], w_f1[0], f1w_in)
            load(wq[:], w_q[0], wq_in)
            load(x_sb[:, 0:NT // 2, :], x[:, 0:NT // 2, :], x_in[0])
            load(ident[:], identity, ident_in)
            load(x_sb[:, NT // 2:, :], x[:, NT // 2:, :], x_in[1])
            load(wkr[:], w_kr[0], wkr_in)
            load(wo[:], w_o[0], wo_in)
            load(ffn_raw[:], w_ffn, ffn_in)
            load(rowo[:], rows_o.partition_broadcast(P), small_in)
            load(gate[:], gates.partition_broadcast(P), small_in)

            def copy_queries(e_pair, b):
                wait(sp, qhi_set, 4 * e_pair + b + 1)
                sp.dma_start(q_hm[0:DC, b].bitcast(F32), q_hl[0:DC, b].bitcast(F32)).then_inc(qhm_in[b], 16)

            def put_maxima(e_pair, b):
                wait(sp, mxt_set, 4 * e_pair + b + 1)
                sp.dma_start(q_hm[DC:DC + 1, b].bitcast(F32).rearrange("o h (c s) -> o (h c) s", c=SC),
                             mxt[:, b, :].bitcast(F32)).then_inc(mrow_in[b], 16)

            def reload(buf, src, used, n, landed):
                wait(sp, used, n)
                load(buf, src, landed)

            reload(f1w[:], w_f1[1], f1_done, 1, f1w_in)
            reload(wq[:], w_q[1], f2_done, 1, wq_in)
            reload(wkr[:], w_kr[1], f3_done, 1, wkr_in)
            reload(wo[:], w_o[1], nf_done, 1, wo_in)
            for b in range(3):
                copy_queries(0, b)
            reload(f1w[:], w_f1[2], f1_done, 2, f1w_in)
            reload(wq[:], w_q[2], f2_done, 2, wq_in)
            put_maxima(0, 0)
            put_maxima(0, 1)

            def step(p):
                for b in range(B):
                    if is_at_most(p, NP - 2) or b + 3 < B:
                        copy_queries(p + (b + 3) // B, (b + 3) % B)
                    if is_at_most(p, NP - 2) or b + 2 < B:
                        put_maxima(p + (b + 2) // B, (b + 2) % B)
                    if b == 0 and is_at_most(p, NP - 3):
                        reload(wkr[:], w_kr[p + 2], f3_done, p + 2, wkr_in)
                    if b == 1 and is_at_most(p, NP - 3):
                        reload(wo[:], w_o[p + 2], nf_done, p + 2, wo_in)
                    if b == 2 and is_at_most(p, NP - 4):
                        reload(f1w[:], w_f1[p + 3], f1_done, p + 3, f1w_in)
                    if b == 3 and is_at_most(p, NP - 4):
                        reload(wq[:], w_q[p + 3], f2_done, p + 3, wq_in)

            step(0)
            with sp.Fori(1, NP - 3) as p:
                step(p)
            step(NP - 3)
            step(NP - 2)
            step(NP - 1)

            for t in range(NT):
                sp.wait_ge(y_set, t + 1)
                sp.dma_start(out[:, t, :], y[:, t % 2, :]).then_inc(y_out[t % 2], 16)
            for i in range(2):
                sp.wait_ge(y_out[i], 16 * (NT // 2))

        @block.gpsimd
        def _(gp):
            gp.dma_start(kvt[:], kv_cols).then_inc(kvt_in, 16)
            gp.dma_start(ropet[:], rope_cols).then_inc(rope_in, 16)
            gp.dma_start(kvn[:], kv_rows).then_inc(kvn_in, 16)
            gp.dma_start(ropen[:], rope_rows).then_inc(rope_in, 16)
            gp.wait_ge(kvt_in, 16)
            gp.wait_ge(rope_in, 32)
            for part, dst in ((0, kt), (1, kt2)):
                nc.gpsimd.tensor_tensor(dst[:].rearrange("p (b s) -> p b s", b=B),
                                        kvt[:, part, :].rearrange("p (b s) -> p b s", b=B),
                                        ropet[:, part, :].unsqueeze(1).broadcast_to([P, B, S]),
                                        ALU.mult).then_inc(pool, 1)
            gp.wait_ge(pool, 2)
            nc.gpsimd.tensor_tensor(kt[:], kt[:], kt2[:], ALU.add).then_inc(kt_set, 1)
            gp.wait_ge(kvn_in, 16)
            for part, dst in ((0, vn), (1, vn2)):
                nc.gpsimd.tensor_tensor(dst[:].rearrange("p (b c) d -> p b (c d)", b=B),
                                        kvn[:, part, :].rearrange("p (b n) -> p b n", b=B),
                                        ropen[:, part, :].unsqueeze(1).broadcast_to([P, B, SC * DC]),
                                        ALU.mult).then_inc(pool, 1)
            gp.wait_ge(pool, 4)
            nc.gpsimd.tensor_tensor(vn[:], vn[:], vn2[:], ALU.add).then_inc(vn_set, 1)
            gp.wait_ge(vmax_set, 1)
            nc.gpsimd.partition_all_reduce(vall[:], vmax[:], P, RMAX).then_inc(vall_set, 1)

            def step(p):
                for b in range(B):
                    g = 4 * p + b
                    wait(gp, phi_set, g + 1)
                    wait(gp, pv_done, g - 3)
                    nc.gpsimd.tensor_tensor(p_lo[:, b].rearrange("p j h s -> p (j h s)"), p_f32[:, b % 2, :],
                                            p_hi[:, b].rearrange("p j h s -> p (j h s)"),
                                            ALU.subtract).then_inc(plo_set, 1)

            pairs(gp, step)
            for t in range(NT):
                gp.wait_ge(x1_set, t + 1)
                gp.wait_ge(const_set, 1)
                if t >= 2:
                    gp.wait_ge(y_set, t - 1)
                nc.gpsimd.tensor_tensor(x1b[:, t % 2, :], x1[:, t % 2, :], gbias[:], ALU.add).then_inc(x1b_set, 1)

        @block.scalar
        def _(act):
            def fold_g(p):
                wait(act, f1_done, p + 1)
                nc.scalar.activation(g_sb[:], ps_f[:, 0:P], ACT.Copy).then_inc(g_set, 1)

            def fold_mt(p):
                wait(act, f2_done, p + 1)
                nc.scalar.activation(mt_sb[:], ps_f[:, 0:DM], ACT.Copy).then_inc(mtsb_set, 1)

            def fold_m(p):
                wait(act, f3_done, p + 1)
                nc.scalar.activation(m_hi[:], ps_f[:, 0:DM].rearrange("p (c n) -> p c n", c=IC),
                                     ACT.Copy).then_inc(mhi_set, 1)

            def fold_n(p):
                wait(act, nf_done, p + 1)
                nc.scalar.activation(n_hi[:, p, :], ps_f[:, 0:DM], ACT.Copy).then_inc(nhi_set, 1)

            def queries_high(p, b):
                wait(act, q_done, 4 * p + b + 1)
                wait(act, st_done, 4 * p + b - 3)
                for h in range(2):
                    ins = nc.scalar.activation(q_hl[0:DC, b, h, :],
                                               ps_a[DC * h:DC * h + DC, 0:S], ACT.Copy)
                ins.then_inc(qhi_set, 1)

            def maxima_row(p, b):
                wait(act, mt_done, 4 * p + b + 1)
                nc.scalar.activation(mxt[:, b, :], ps_s[0:4, 0, 0:P], ACT.Copy).then_inc(mxt_set, 1)

            def exps(p, b):
                g = 4 * p + b
                scores_t = ps_t[:, b % 2, :, :].rearrange("p j n -> p (j n)")
                wait(act, st_done, g + 1)
                wait(act, plo_set, g - 1)
                nc.scalar.activation(p_f32[:, b % 2, :], scores_t, ACT.Exp).then_inc(p32_set, 1)
                if b == 0 and is_at_most(p, NP - 2):
                    fold_m(p + 1)
                if b == 1 and is_at_most(p, NP - 2):
                    fold_n(p + 1)
                if b == 2 and is_at_most(p, NP - 3):
                    fold_g(p + 2)
                if b == 3 and is_at_most(p, NP - 3):
                    fold_mt(p + 2)
                if is_at_most(p, NP - 2) or b + 2 < B:
                    maxima_row(p + (b + 2) // B, (b + 2) % B)
                wait(act, pv_done, g - 3)
                nc.scalar.activation(p_hi[:, b].rearrange("p j h s -> p (j h s)"), scores_t,
                                     ACT.Exp).then_inc(phi_set, 1)

            def deviation(i):
                act.wait_ge(var_set, i + 1)
                half = slice(i * NT // 2, (i + 1) * NT // 2)
                nc.scalar.activation(std[:, half], mv[:, half, 1], ACT.Sqrt, bias=eps[:, 0:1]).then_inc(std_set, 1)

            fold_g(0)
            deviation(0)
            fold_mt(0)
            deviation(1)
            fold_m(0)
            fold_n(0)
            act.wait_ge(small_in, 32)
            nc.scalar.activation(tanhs[:], gate[:], ACT.Tanh).then_inc(tanh_set, 1)
            for i in range(2):
                act.wait_ge(xt_done, i + 1)
                nc.scalar.activation(xt_hi[:, :, i * T // 2:(i + 1) * T // 2], ps_t[:, i], ACT.Copy).then_inc(xthi_set, 1)
            act.wait_ge(kt_set, 1)
            nc.scalar.activation(k_hi[:], kt[:], ACT.Copy).then_inc(khi_set, 1)
            for b in range(3):
                queries_high(0, b)
            fold_g(1)
            fold_mt(1)
            for b in range(2):
                maxima_row(0, b)

            def step(p):
                for b in range(B):
                    if is_at_most(p, NP - 2) or b + 3 < B:
                        queries_high(p + (b + 3) // B, (b + 3) % B)
                    exps(p, b)

            pairs(act, step)

            def context_high(t):
                act.wait_ge(ctt_done, t + 1)
                if t >= 2:
                    act.wait_ge(o_done, t - 1)
                nc.scalar.activation(ct_hi[:, t % 2].rearrange("p a b -> p (a b)"),
                                     ps_t[:, t % 2].rearrange("p j n -> p (j n)"), ACT.Copy).then_inc(cthi_set, 1)

            def normed_copy(t):
                act.wait_ge(xt2_done, t + 1)
                if t >= 2:
                    act.wait_ge(ffn_done, t - 1)
                nc.scalar.activation(xt2[:, t % 2].rearrange("p c n -> p (c n)"), ps_s[:, 0, 0:DM], ACT.Copy).then_inc(xt2_set, 1)

            context_high(0)
            for t in range(NT):
                if t + 1 < NT:
                    context_high(t + 1)
                act.wait_ge(var2_set, t + 1)
                nc.scalar.activation(sd2[:, t % 2:t % 2 + 1], mv2[:, t % 2, 1:2], ACT.Sqrt,
                                     bias=eps[:, 0:1]).then_inc(std2_set, 1)
                normed_copy(t)

        @block.vector
        def _(v):
            chain = [0]

            def link(ins):
                chain[0] += 1
                ins.then_inc(dve, 1)
                v.wait_ge(dve, chain[0])

            def split_low(out_, whole, high, done):
                nc.vector.tensor_tensor(out_, whole, high, ALU.subtract).then_inc(done, 1)

            def fold_m(p):
                wait(v, mhi_set, p + 1)
                split_low(m_lo[:], ps_f[:, 0:DM].rearrange("p (c n) -> p c n", c=IC), m_hi[:].bitcast(F32), mlo_set)

            def fold_n(p):
                wait(v, nhi_set, p + 1)
                split_low(n_lo[:, p, :], ps_f[:, 0:DM], n_hi[:, p, :].bitcast(F32), nlo_set)

            nc.vector.memset(k_lo[DC:DC + 1, :].bitcast(F32), -1.0)
            nc.vector.memset(eps[:], EPS)
            link(nc.vector.memset(v_hi[:], 1.0))
            for i in range(2):
                tiles = range(i * NT // 2, (i + 1) * NT // 2)
                v.wait_ge(x_in[i], 16)
                for t in tiles:
                    ins = nc.vector.bn_stats(stats[:, t, :], x_sb[:, t, :])
                link(ins)
                for t in tiles:
                    ins = nc.vector.bn_aggr(mv[:, t, :], stats[:, t, :])
                ins.then_inc(var_set, 1)
                half = slice(i * NT // 2, (i + 1) * NT // 2)
                v.wait_ge(std_set, i + 1)
                link(nc.vector.reciprocal(rstd[:, half], std[:, half]))
                for t in tiles:
                    nc.vector.tensor_scalar(xn[:, t, :], x_sb[:, t, :], mv[:, t, 0:1], rstd[:, t:t + 1],
                                            ALU.subtract, ALU.mult).then_inc(xn_set, 1)
            fold_m(0)
            fold_n(0)
            for i in range(2):
                v.wait_ge(xthi_set, i + 1)
                rows = slice(i * T // 2, (i + 1) * T // 2)
                split_low(xt_lo[:, :, rows], ps_t[:, i], xt_hi[:, :, rows].bitcast(F32), xtlo_set)
            v.wait_ge(khi_set, 1)
            split_low(k_lo[0:DC, :], kt[0:DC, :], k_hi[0:DC, :].bitcast(F32), klo_set)

            def queries_low(p, b):
                wait(v, qhi_set, 4 * p + b + 1)
                for h in range(2):
                    ins = nc.vector.tensor_tensor(q_hl[DC:P, b, h, :], ps_a[DC * h:DC * h + DC, 0:S],
                                                  q_hl[0:DC, b, h, :].bitcast(F32), ALU.subtract)
                ins.then_inc(qlo_set, 1)

            def maxima(p, b):
                e = 4 * p + b
                wait(v, s_done, e + 1)
                nc.vector.tensor_reduce(mx[:, b, :], ps_s[:].rearrange("p h (c l) -> p (h c) l", c=SC),
                                        AX_X, ALU.max).then_inc(max_set, 1)

            def context(p, b):
                g = 4 * p + b
                cs = ps_c[:, 0:4 * (DC + 1)].rearrange("p (n d) -> p n d", n=4)
                wait(v, pv_done, g + 1)
                nc.vector.reciprocal(rden[:, b, :], cs[:, :, DC]).then_inc(rec_set, 1)
                wait(v, rec_set, g + 1)
                nc.vector.tensor_tensor(cx[:, SC * b:SC * b + SC, p, :].rearrange("p c (h d) -> p h c d", h=2),
                                        cs[:, :, 0:DC].rearrange("p (h c) d -> p h c d", h=2),
                                        rden[:, b, :].rearrange("p (h c) -> p h c", h=2).unsqueeze(3)
                                        .broadcast_to([P, 2, SC, DC]), ALU.mult).then_inc(cx_set, 1)

            queries_low(0, 0)
            queries_low(0, 1)
            queries_low(0, 2)
            v.wait_ge(vn_set, 1)
            nc.vector.tensor_reduce(vmax[:], vn[:], mybir.AxisListType.XY, ALU.max,
                                    apply_absolute_value=True).then_inc(vmax_set, 1)
            maxima(0, 0)
            maxima(0, 1)
            v.wait_ge(vall_set, 1)
            link(nc.vector.tensor_scalar(vinv[:], vall[:], TINY, 1.0 / V_TOP, ALU.max, ALU.mult))
            link(nc.vector.reciprocal(vscale[:], vinv[:]))
            link(nc.vector.tensor_scalar(vn2[:], vn[:], vscale[:, 0:1], None, ALU.mult))
            link(nc.vector.tensor_copy(v_hi[:, :, 0:DC], vn2[:]))
            nc.vector.tensor_tensor(v_lo[:], vn2[:], v_hi[:, :, 0:DC], ALU.subtract).then_inc(v_set, 1)
            v.wait_ge(tanh_set, 1)
            v.wait_ge(ffn_in, 16)
            nc.vector.tensor_tensor(ga[:], tanhs[:, 0:1], vinv[:], ALU.mult)
            link(nc.vector.tensor_scalar(wffn[:], ffn_raw[:], tanhs[:, 1:2], None, ALU.mult))
            nc.vector.tensor_tensor(wffn[:], wffn[:], rowo[:, 0, :].unsqueeze(1).broadcast_to([P, IC, DM]), ALU.mult)
            nc.vector.tensor_scalar(gbias[:], rowo[:, 1, :], tanhs[:, 1:2], None, ALU.mult).then_inc(const_set, 1)

            def step(p):
                for b in range(B):
                    if is_at_most(p, NP - 2) or b + 2 < B:
                        maxima(p + (b + 2) // B, (b + 2) % B)
                    if is_at_most(p, NP - 2) or b + 3 < B:
                        queries_low(p + (b + 3) // B, (b + 3) % B)
                    if b >= 2:
                        context(p, b - 2)
                    elif not isinstance(p, int) or p > 0:
                        context(p - 1, b + 2)
                    if b == 0 and is_at_most(p, NP - 2):
                        fold_m(p + 1)
                    if b == 1 and is_at_most(p, NP - 2):
                        fold_n(p + 1)

            pairs(v, step)
            for b in range(2, B):
                context(NP - 1, b)

            def context_low(t):
                v.wait_ge(cthi_set, t + 1)
                if t >= 2:
                    v.wait_ge(o_done, t - 1)
                nc.vector.tensor_tensor(ct_lo[:, t % 2].rearrange("p a b -> p (a b)"),
                                        ps_t[:, t % 2].rearrange("p j n -> p (j n)"),
                                        ct_hi[:, t % 2].rearrange("p a b -> p (a b)").bitcast(F32),
                                        ALU.subtract).then_inc(ctlo_set, 1)

            def residual(t):
                i = t % 2
                v.wait_ge(o_done, t + 1)
                nc.vector.scalar_tensor_tensor(out=x1[:, i, :], in0=ps_o(t), scalar=ga[:, 0:1], in1=x_sb[:, t, :],
                                               op0=ALU.mult, op1=ALU.add).then_inc(x1_set, 1)
                v.wait_ge(x1_set, t + 1)
                link(nc.vector.bn_stats(st2[:, i, :], x1[:, i, :]))
                nc.vector.bn_aggr(mv2[:, i, :], st2[:, i, :]).then_inc(var2_set, 1)
                v.wait_ge(std2_set, t + 1)
                link(nc.vector.reciprocal(rs2[:, i:i + 1], sd2[:, i:i + 1]))
                nc.vector.tensor_scalar(xn2[:, i, :], x1[:, i, :], mv2[:, i, 0:1], rs2[:, i:i + 1],
                                        ALU.subtract, ALU.mult).then_inc(xn2_set, 1)

            def result(t):
                v.wait_ge(ffn_done, t + 1)
                v.wait_ge(x1b_set, t + 1)
                if t >= 2:
                    v.wait_ge(y_out[t % 2], 16 * (t // 2))
                nc.vector.tensor_tensor(y[:, t % 2, :], ps_s[:, 1, 0:DM], x1b[:, t % 2, :], ALU.add).then_inc(y_set, 1)

            context_low(0)
            for t in range(NT):
                if t + 1 < NT:
                    context_low(t + 1)
                residual(t)
                if t >= 1:
                    result(t - 1)
            result(NT - 1)

        @block.tensor
        def _(pe):
            def mm(o, lhsT, rhs, first, last):
                return nc.tensor.matmul(o, lhsT=lhsT, rhs=rhs, start=first, stop=last)

            def fold_1(p):
                wait(pe, f1w_in, 16 * (p + 1))
                kcq = f1w[:, 0:2 * 2 * K].rearrange("q (c h k) -> q c h k", c=2, h=2)
                wqr = f1w[:, 2 * 2 * K:].rearrange("q (c h r) -> q c h r", c=2, h=2)
                for h in range(2):
                    for c in range(2):
                        ins = mm(ps_f[:, R * h:R * h + R], kcq[:, c, h, :], wqr[:, c, h, :], c == 0, c == 1)
                ins.then_inc(f1_done, 1)

            def fold_2(p):
                wait(pe, g_set, p + 1)
                wait(pe, wq_in, 16 * (p + 1))
                for h in range(2):
                    ins = mm(ps_f[R * h:R * h + R, 0:DM], g_sb[:, R * h:R * h + R], wq[:, h, :], True, True)
                ins.then_inc(f2_done, 1)

            def fold_3(p):
                wait(pe, mtsb_set, p + 1)
                wait(pe, wkr_in, 16 * (p + 1))
                for c in range(IC):
                    ins = mm(ps_f[:, P * c:P * c + P], mt_sb[:, P * c:P * c + P], wkr[:], True, True)
                ins.then_inc(f3_done, 1)

            def fold_n(p):
                wait(pe, wo_in, 16 * (p + 1))
                for h in range(2):
                    ins = mm(ps_f[DC * h:DC * h + DC, 0:DM], wo[:, DC * h:DC * h + DC],
                             wo[:, 2 * DC + DM * h:2 * DC + DM * h + DM], True, True)
                ins.then_inc(nf_done, 1)

            def queries(p, b):
                wait(pe, mlo_set, p + 1)
                rows = slice(b * S, (b + 1) * S)
                n = 0
                for c in range(IC):
                    for w, xt in ((m_hi, xt_hi), (m_hi, xt_lo), (m_lo, xt_hi)):
                        ins = mm(ps_a[:, 0:S], w[:, c, :], xt[:, c, rows], n == 0, n == 3 * IC - 1)
                        n += 1
                ins.then_inc(q_done, 1)

            def scores(p, b):
                wait(pe, qlo_set, 4 * p + b + 1)
                wait(pe, mxt_set, 4 * p + b)
                for h in range(2):
                    for c in range(SC):
                        ins = mm(ps_s[:, h, S * c:S * c + S], q_hl[:, b, h, P * c:P * c + P],
                                 k_hi[:, b * S:(b + 1) * S], True, True)
                ins.then_inc(s_done, 1)

            def scores_t(p, b):
                g = 4 * p + b
                wait(pe, qhm_in[b], 16 * (p + 1))
                wait(pe, mrow_in[b], 16 * (p + 1))
                wait(pe, phi_set, g - 1)
                for j in range(SC):
                    keys = slice(b * S + P * j, b * S + P * j + P)
                    o = ps_t[:, b % 2, j, :]
                    mm(o, k_hi[:, keys], q_hl[:, b].rearrange("k h s -> k (h s)"), True, False)
                    ins = mm(o, k_lo[:, keys], q_hm[:, b].rearrange("k h s -> k (h s)"), False, True)
                ins.then_inc(st_done, 1)

            def turn_maxima(p, b):
                wait(pe, max_set, 4 * p + b + 1)
                nc.tensor.transpose(ps_s[0:4, 0, 0:P], mx[:, b, :], ident[:]).then_inc(mt_done, 1)

            def values(p, b):
                g = 4 * p + b
                wait(pe, plo_set, g + 1)
                wait(pe, cx_set, g)
                for h in range(2):
                    for c in range(SC):
                        at = (2 * h + c) * (DC + 1)
                        for j in range(SC):
                            ph = p_hi[:, b, j, h, P * c:P * c + P]
                            pl = p_lo[:, b, j, h, P * c:P * c + P]
                            vh, vl = v_hi[:, SC * b + j, :], v_lo[:, SC * b + j, :]
                            mm(ps_c[:, at:at + DC + 1], ph, vh, j == 0, False)
                            mm(ps_c[:, at:at + DC], ph, vl, False, False)
                            ins = mm(ps_c[:, at:at + DC + 1], pl, vh, False, j == SC - 1)
                ins.then_inc(pv_done, 1)

            fold_1(0)
            fold_2(0)
            fold_3(0)
            pe.wait_ge(mlo_set, 1)
            fold_n(0)
            pe.wait_ge(ident_in, 16)
            for i in range(2):
                for t in range(NT // 2):
                    pe.wait_ge(xn_set, i * NT // 2 + t + 1)
                    for c in range(IC):
                        ins = nc.tensor.transpose(ps_t[:, i, c, P * t:P * t + P],
                                                  xn[:, i * NT // 2 + t, P * c:P * c + P], ident[:])
                ins.then_inc(xt_done, 1)
            pe.wait_ge(xtlo_set, 1)
            queries(0, 0)
            pe.wait_ge(qlo_set, 1)
            queries(0, 1)
            pe.wait_ge(qlo_set, 2)
            pe.wait_ge(xtlo_set, 2)
            queries(0, 2)
            pe.wait_ge(nlo_set, 1)
            fold_1(1)
            fold_2(1)
            pe.wait_ge(klo_set, 1)
            pe.wait_ge(mtsb_set, 2)
            for b in range(2):
                scores(0, b)
                turn_maxima(0, b)

            def step(p):
                for b in range(B):
                    if is_at_most(p, NP - 2) or b + 3 < B:
                        wait(pe, qlo_set, 4 * p + b + 3)
                        queries(p + (b + 3) // B, (b + 3) % B)
                    if is_at_most(p, NP - 2) or b + 2 < B:
                        if b == 0 and is_at_most(p, NP - 2):
                            wait(pe, mtsb_set, p + 2)
                        if b == 1 and is_at_most(p, NP - 2):
                            wait(pe, mlo_set, p + 2)
                        if b == 2:
                            wait(pe, nlo_set, p + 2)
                        if b == 3 and is_at_most(p, NP - 3):
                            wait(pe, g_set, p + 3)
                        scores(p + (b + 2) // B, (b + 2) % B)
                    scores_t(p, b)
                    if isinstance(p, int) and p == 0 and b == 2:
                        pe.wait_ge(v_set, 1)
                    if b >= 2:
                        values(p, b - 2)
                    elif not isinstance(p, int) or p > 0:
                        values(p - 1, b + 2)
                    if is_at_most(p, NP - 2 if b < 2 else NP - 3):
                        wait(pe, max_set, 4 * p + b + 3)
                        (fold_3, fold_n, fold_1, fold_2)[b](p + 1 if b < 2 else p + 2)
                    if is_at_most(p, NP - 2) or b + 2 < B:
                        turn_maxima(p + (b + 2) // B, (b + 2) % B)

            pairs(pe, step)
            values(NP - 1, B - 2)
            values(NP - 1, B - 1)

            def turn_context(t):
                if t >= 2:
                    pe.wait_ge(ctlo_set, t - 1)
                for p in range(NP):
                    ins = nc.tensor.transpose(ps_t[:, t % 2, p // 4, P * (p % 4):P * (p % 4) + P],
                                              cx[:, t, p, :], ident[:])
                ins.then_inc(ctt_done, 1)

            def project(t):
                pe.wait_ge(ctlo_set, t + 1)
                if t >= 2:
                    pe.wait_ge(x1_set, t - 1)
                n = 0
                for p in range(NP):
                    for c, w in ((ct_hi, n_hi), (ct_hi, n_lo), (ct_lo, n_hi)):
                        ins = mm(ps_o(t), c[:, t % 2, p, :], w[:, p, :], n == 0, n == 3 * NP - 1)
                        n += 1
                ins.then_inc(o_done, 1)

            def linear(t):
                pe.wait_ge(xn2_set, t + 1)
                if t >= 1:
                    pe.wait_ge(xt2_set, t)
                for c in range(IC):
                    ins = nc.tensor.transpose(ps_s[:, 0, P * c:P * c + P], xn2[:, t % 2, P * c:P * c + P], ident[:])
                ins.then_inc(xt2_done, 1)

            def linear_mm(t):
                pe.wait_ge(xt2_set, t + 1)
                if t >= 1:
                    pe.wait_ge(y_set, t)
                for c in range(IC):
                    ins = mm(ps_s[:, 1, 0:DM], xt2[:, t % 2, c, :], wffn[:, c, :], c == 0, c == IC - 1)
                ins.then_inc(ffn_done, 1)

            pe.wait_ge(phi_set, STEPS)
            pe.wait_ge(cx_set, STEPS)
            pe.wait_ge(const_set, 1)
            turn_context(0)
            for t in range(NT):
                if t + 1 < NT:
                    turn_context(t + 1)
                if t >= 1:
                    linear(t - 1)
                project(t)
                if t >= 1:
                    linear_mm(t - 1)
            linear(NT - 1)
            linear_mm(NT - 1)


def _rope():
    import numpy as np
    inv = (1.0 / np.power(np.float32(10000.0), np.arange(0, DC, 2, dtype=np.float32) / np.float32(DC))).astype(np.float32)
    f = (np.arange(S, dtype=np.float32)[:, None] * inv[None, :]).astype(np.float32).astype(np.float64)
    sin, cos = np.repeat(np.sin(f), 2, -1), np.repeat(np.cos(f), 2, -1)
    sin[:, :DC // 2] *= -1.0
    return np.stack([cos, sin]).astype(np.float32)


def kernel(x, ctx_512, g_xattn, g_ffn, L0_xattn_Wq, L0_xattn_w_kc_q, L0_xattn_w_kc_kv, L0_xattn_W_qr,
           L0_xattn_W_kr, L0_xattn_Wo, L0_ffn_weight, L0_ffn_scale_weight, L0_ffn_bias):
    import numpy as np
    import concourse.bacc as bacc
    from concourse.bass_utils import run_bass_kernel_spmd

    A = lambda a: np.ascontiguousarray(np.asarray(a))
    kv = A(ctx_512)
    swapped = np.concatenate([kv[..., DC // 2:], kv[..., :DC // 2]], -1)
    both = np.stack([kv, swapped]).reshape(2, NT, P, DC)
    rope = _rope()
    Wq, kcq, kckv = A(L0_xattn_Wq), A(L0_xattn_w_kc_q), A(L0_xattn_w_kc_kv)
    Wqr, Wkr, Wo = A(L0_xattn_W_qr), A(L0_xattn_W_kr), A(L0_xattn_Wo)
    kcq_t = kcq.reshape(NP, 2, K, 2, QC).transpose(0, 4, 3, 1, 2).reshape(NP, QC, 4 * K)
    wqr_t = Wqr.reshape(NP, 2, 2, QC, R).transpose(0, 3, 2, 1, 4).reshape(NP, QC, 4 * R)
    wkr_bd = np.zeros((NP, 2, R, 2, DC), np.float32)
    for h in range(2):
        wkr_bd[:, h, :, h, :] = Wkr.reshape(NP, 2, DC, R)[:, h].transpose(0, 2, 1)
    kckv_t = kckv.reshape(NP, 2, K, DC).transpose(0, 2, 1, 3).reshape(NP, K, 2 * DC)
    wo_t = Wo.T.reshape(NP, 2, K, DM).transpose(0, 2, 1, 3).reshape(NP, K, 2 * DM)
    arrays = {
        "x_rows": A(x).reshape(NT, P, DM),
        "kv_rows": both.transpose(2, 0, 1, 3).reshape(P, 2, NT * DC),
        "kv_cols": np.tile(both.reshape(2, T, DC).transpose(2, 0, 1), (2, 1, 1)),
        "rope_rows": rope.reshape(2, SC, P, DC).transpose(2, 0, 1, 3).reshape(P, 2, SC * DC),
        "rope_cols": np.tile(rope.transpose(2, 0, 1), (2, 1, 1)),
        "identity": np.eye(P, dtype=np.float32),
        "w_f1": np.concatenate([kcq_t, wqr_t], -1),
        "w_q": Wq.reshape(NP, 2, K, DM).transpose(0, 2, 1, 3),
        "w_kr": wkr_bd.reshape(NP, P, P),
        "w_o": np.concatenate([kckv_t, wo_t], -1),
        "w_ffn": A(L0_ffn_weight).T.reshape(IC, P, DM).transpose(1, 0, 2),
        "rows_o": np.stack([A(L0_ffn_scale_weight), A(L0_ffn_bias)]),
        "gates": np.concatenate([A(g_xattn).reshape(1), A(g_ffn).reshape(1)]),
    }
    arrays = {f"{n}_dram": np.ascontiguousarray(a) for n, a in arrays.items()}
    nc = bacc.Bacc("TRN2", target_bir_lowering=False, num_devices=1)
    aps = [nc.dram_tensor(n, a.shape, mybir.dt.from_np(a.dtype), kind="ExternalInput").ap() for n, a in arrays.items()]
    aps[0] = aps[0].rearrange("t p n -> p t n")
    out = nc.dram_tensor("out_dram", (NT, P, DM), F32, kind="ExternalOutput").ap()
    flamingo_kernel(nc, *aps, out.rearrange("t p n -> p t n"))
    r = run_bass_kernel_spmd(nc, [arrays], core_ids=[0])
    return r.results[0]["out_dram"].reshape(B, S, DM)
```

```python
from contextlib import ExitStack

import concourse.bass as bass
from concourse import mybir

P = 128
F32 = mybir.dt.float32
F32R = mybir.dt.float32r
F16 = mybir.dt.float16
ACT = mybir.ActivationFunctionType
ALU = mybir.AluOpType
AX_X = mybir.AxisListType.X
RMAX = bass.bass_isa.ReduceOp.max

B, S, DM = 4, 256, 256
H, K, DC, DQ, R = 16, 128, 64, 192, 64
T = B * S
NT = T // P
NP = H // 2
STEPS = NP * B
IC = DM // P
SC = S // P
QC = 96
EPS = 1e-5
V_TOP = 1024.0
TINY = 1e-20


def flamingo_kernel(nc, x, kv_rope, identities, w_f1, w_q, w_kr, w_o,
                    w_ffn, rows_o, gates, out):
    ctx = ExitStack()
    with ctx:
        def sb(name, shape, dt=F32):
            return ctx.enter_context(nc.sbuf_tensor(name, shape, dt))

        def pb(name, shape):
            return ctx.enter_context(nc.psum_tensor(name, shape, F32))

        def sem(name):
            return ctx.enter_context(nc.semaphore(name))

        x_sb = sb("x_sb", [P, NT, DM])
        kvr = sb("kvr", [P, T + S])
        idents = sb("idents", [P, 2, P])
        f1w = sb("f1w", [QC, 2 * 2 * K + 2 * 2 * R])
        wq = sb("wq", [P, 2, DM])
        wkr = sb("wkr", [P, P])
        wo = sb("wo", [P, 2 * DC + 2 * DM])
        ffn_raw = sb("ffn_raw", [P, IC, DM])
        rowo = sb("rowo", [P, 2, DM])
        gate = sb("gate", [P, 2])
        stats = sb("stats", [P, NT, 6])
        mv = sb("mv", [P, NT, 2])
        std = sb("std", [P, NT])
        rstd = sb("rstd", [P, NT])
        eps = sb("eps", [P, 1])
        warm = sb("warm", [P, 1])
        xn = sb("xn", [P, NT, DM])
        xt_hi = sb("xt_hi", [P, IC, T], F32R)
        xt_lo = sb("xt_lo", [P, IC, T], F32R)
        turned = sb("turned", [P, T])
        k_hi = sb("k_hi", [P, T], F32R)
        k_lo = sb("k_lo", [DC + 1, T], F32R)
        v_hi = sb("v_hi", [P, NT, DC + 1], F16)
        v_lo = sb("v_lo", [P, NT, DC], F16)
        vmax = sb("vmax", [P, 1])
        vall = sb("vall", [P, 1])
        vinv = sb("vinv", [P, 1])
        vscale = sb("vscale", [P, 1])
        tanhs = sb("tanhs", [P, 2])
        ga = sb("ga", [P, 1])
        wffn = sb("wffn", [P, IC, DM])
        gbias = sb("gbias", [P, DM])
        g_sb = sb("g_sb", [P, P])
        mt_sb = sb("mt_sb", [P, DM])
        m_hi = sb("m_hi", [P, IC, P], F32R)
        m_lo = sb("m_lo", [P, IC, P], F32R)
        n_hi = sb("n_hi", [P, NP, DM], F32R)
        n_lo = sb("n_lo", [P, NP, DM], F32R)
        q_hl = sb("q_hl", [P, B, 2, S], F32R)
        q_hm = sb("q_hm", [DC + 1, B, 2, S], F32R)
        mx = sb("mx", [P, B, 4])
        mxt = sb("mxt", [4, B, P], F32R)
        p_f32 = sb("p_f32", [P, 2, 4 * S])
        p_hi = sb("p_hi", [P, B, SC, 2, S], F16)
        p_lo = sb("p_lo", [P, B, SC, 2, S], F16)
        rden = sb("rden", [P, B, 4])
        cx = sb("cx", [P, NT, NP, P])
        ct_hi = sb("ct_hi", [P, 2, NP, P], F32R)
        ct_lo = sb("ct_lo", [P, 2, NP, P], F32R)
        x1 = sb("x1", [P, 2, DM])
        x1b = sb("x1b", [P, 2, DM])
        xn2 = sb("xn2", [P, 2, DM])
        st2 = sb("st2", [P, 2, 6])
        mv2 = sb("mv2", [P, 2, 2])
        sd2 = sb("sd2", [P, 2])
        rs2 = sb("rs2", [P, 2])
        xt2 = sb("xt2", [P, 2, IC, P])
        y = sb("y", [P, 2, DM])

        ps_s = pb("ps_s", [P, 2, 512])
        ps_t = pb("ps_t", [P, 2, SC, 512])
        ps_c = pb("ps_c", [P, 512])
        ps_a = pb("ps_a", [P, 512])
        ps_f = ps_s[:, 1, :]
        ident, ident4 = idents[:, 0, :], idents[:, 1, :]

        def ps_o(t):
            return (ps_c if t % 2 else ps_a)[:, 0:DM]

        def ps_ct(t):
            return (ps_t[:, 0] if t % 2 else ps_s[:]).rearrange("p j n -> p (j n)")

        ps_x2, ps_y = ps_t[:, 1, 0, 0:DM], ps_t[:, 1, 1, 0:DM]

        x_in = [sem(f"x_in{i}") for i in range(3)]
        kvr_in, ident_in, gate_in = sem("kvr_in"), sem("ident_in"), sem("gate_in")
        f1w_in, wq_in, wkr_in, wo_in = sem("f1w_in"), sem("wq_in"), sem("wkr_in"), sem("wo_in")
        ffn_in, small_in = sem("ffn_in"), sem("small_in")
        qhm_in = [sem(f"qhm_in{b}") for b in range(B)]
        mrow_in = [sem(f"mrow_in{b}") for b in range(B)]
        y_out = [sem(f"y_out{i}") for i in range(2)]
        xt_done, f1_done, f2_done, f3_done, nf_done, k_done, v_done = (sem(n) for n in (
            "xt_done", "f1_done", "f2_done", "f3_done", "nf_done", "k_done", "v_done"))
        q_done, s_done, st_done, mt_done, pv_done = (sem(n) for n in (
            "q_done", "s_done", "st_done", "mt_done", "pv_done"))
        ctt_done, o_done, xt2_done, ffn_done = (sem(n) for n in (
            "ctt_done", "o_done", "xt2_done", "ffn_done"))
        xthi_set, khi_set, g_set, mtsb_set, mhi_set, nhi_set = (sem(n) for n in (
            "xthi_set", "khi_set", "g_set", "mtsb_set", "mhi_set", "nhi_set"))
        qhi_set, p32_set, phi_set, mxt_set = (sem(n) for n in ("qhi_set", "p32_set", "phi_set", "mxt_set"))
        std_set, std2_set = sem("std_set"), sem("std2_set")
        tanh_set, vhi_set, cthi_set, xt2_set = (sem(n) for n in ("tanh_set", "vhi_set", "cthi_set", "xt2_set"))
        dve = sem("dve")
        xn_set, xtlo_set, klo_set, vinv_set, v_set, mlo_set, nlo_set = (sem(n) for n in (
            "xn_set", "xtlo_set", "klo_set", "vinv_set", "v_set", "mlo_set", "nlo_set"))
        max_set, qlo_set, plo_set, cx_set = (sem(n) for n in ("max_set", "qlo_set", "plo_set", "cx_set"))
        vmax_set, const_set, ctlo_set, x1_set, xn2_set, y_set = (sem(n) for n in (
            "vmax_set", "const_set", "ctlo_set", "x1_set", "xn2_set", "y_set"))
        rec_set, var_set, var2_set, eps_set = (sem(n) for n in ("rec_set", "var_set", "var2_set", "eps_set"))
        pool = sem("pool")
        turned_set, vall_set, x1b_set = sem("turned_set"), sem("vall_set"), sem("x1b_set")

        def wait(eng, s, n):
            if not isinstance(n, int) or n > 0:
                eng.wait_ge(s, n)

        def pairs(eng, step):
            step(0)
            with eng.Fori(1, NP - 2) as p:
                step(p)
            step(NP - 2)
            step(NP - 1)

        def is_at_most(p, last):
            return p <= last if isinstance(p, int) else True

        block = ctx.enter_context(nc.Block())

        @block.sync
        def _(sp):
            def load(buf, src, landed):
                sp.dma_start(buf, src).then_inc(landed, 16)

            load(x_sb[:, 0:2, :], x[:, 0:2, :], x_in[0])
            load(f1w[:], w_f1[0], f1w_in)
            load(x_sb[:, 2:4, :], x[:, 2:4, :], x_in[1])
            load(wq[:], w_q[0], wq_in)
            load(idents[:], identities, ident_in)
            load(x_sb[:, 4:, :], x[:, 4:, :], x_in[2])
            load(wkr[:], w_kr[0], wkr_in)
            load(kvr[:], kv_rope, kvr_in)
            load(gate[:], gates.partition_broadcast(P), gate_in)
            load(wo[:], w_o[0], wo_in)

            def copy_queries(e_pair, b):
                wait(sp, qhi_set, 4 * e_pair + b + 1)
                sp.dma_start(q_hm[0:DC, b].bitcast(F32), q_hl[0:DC, b].bitcast(F32)).then_inc(qhm_in[b], 16)

            def put_maxima(e_pair, b):
                wait(sp, mxt_set, 4 * e_pair + b + 1)
                sp.dma_start(q_hm[DC:DC + 1, b].bitcast(F32).rearrange("o h (c s) -> o (h c) s", c=SC),
                             mxt[:, b, :].bitcast(F32)).then_inc(mrow_in[b], 16)

            def reload(buf, src, used, n, landed):
                wait(sp, used, n)
                load(buf, src, landed)

            reload(f1w[:], w_f1[1], f1_done, 1, f1w_in)
            reload(wq[:], w_q[1], f2_done, 1, wq_in)
            reload(wkr[:], w_kr[1], f3_done, 1, wkr_in)
            load(ffn_raw[:], w_ffn, ffn_in)
            load(rowo[:], rows_o.partition_broadcast(P), small_in)
            copy_queries(0, 0)
            copy_queries(0, 1)
            put_maxima(0, 0)
            copy_queries(0, 2)
            reload(wo[:], w_o[1], nf_done, 1, wo_in)
            reload(f1w[:], w_f1[2], f1_done, 2, f1w_in)
            reload(wq[:], w_q[2], f2_done, 2, wq_in)

            def step(p):
                for b in range(B):
                    if is_at_most(p, NP - 2) or b + 3 < B:
                        copy_queries(p + (b + 3) // B, (b + 3) % B)
                    if is_at_most(p, NP - 2) or b + 1 < B:
                        put_maxima(p + (b + 1) // B, (b + 1) % B)
                    if b == 0 and is_at_most(p, NP - 3):
                        reload(wkr[:], w_kr[p + 2], f3_done, p + 2, wkr_in)
                    if b == 1 and is_at_most(p, NP - 3):
                        reload(wo[:], w_o[p + 2], nf_done, p + 2, wo_in)
                    if b == 2 and is_at_most(p, NP - 4):
                        reload(f1w[:], w_f1[p + 3], f1_done, p + 3, f1w_in)
                    if b == 3 and is_at_most(p, NP - 4):
                        reload(wq[:], w_q[p + 3], f2_done, p + 3, wq_in)

            step(0)
            with sp.Fori(1, NP - 3) as p:
                step(p)
            step(NP - 3)
            step(NP - 2)
            step(NP - 1)

            for t in range(NT):
                sp.wait_ge(y_set, t + 1)
                sp.dma_start(out[:, t, :], y[:, t % 2, :]).then_inc(y_out[t % 2], 16)
            for i in range(2):
                sp.wait_ge(y_out[i], 16 * (NT // 2))

        @block.gpsimd
        def _(gp):
            gp.wait_ge(kvr_in, 16)
            for i in range(2):
                rows = slice(i * T // 2, (i + 1) * T // 2)
                nc.gpsimd.tensor_tensor(turned[:, rows].rearrange("p (b s) -> p b s", b=B // 2),
                                        kvr[:, rows].rearrange("p (b s) -> p b s", b=B // 2),
                                        kvr[:, T:].unsqueeze(1).broadcast_to([P, B // 2, S]),
                                        ALU.mult).then_inc(turned_set, 1)
            gp.wait_ge(ffn_in, 16)
            gp.wait_ge(small_in, 16)
            nc.gpsimd.tensor_tensor(wffn[:], ffn_raw[:], rowo[:, 0, :].unsqueeze(1).broadcast_to([P, IC, DM]),
                                    ALU.mult).then_inc(pool, 1)
            gp.wait_ge(vmax_set, 1)
            nc.gpsimd.partition_all_reduce(vall[:], vmax[:], P, RMAX).then_inc(vall_set, 1)
            gp.wait_ge(tanh_set, 1)
            gp.wait_ge(pool, 1)
            nc.gpsimd.tensor_scalar(wffn[:], wffn[:], tanhs[:, 1:2], None, ALU.mult)
            nc.gpsimd.tensor_scalar(gbias[:], rowo[:, 1, :], tanhs[:, 1:2], None, ALU.mult).then_inc(const_set, 1)

            def step(p):
                for b in range(B):
                    g = 4 * p + b
                    wait(gp, phi_set, g + 1)
                    wait(gp, pv_done, g - 3)
                    nc.gpsimd.tensor_tensor(p_lo[:, b].rearrange("p j h s -> p (j h s)"), p_f32[:, b % 2, :],
                                            p_hi[:, b].rearrange("p j h s -> p (j h s)"),
                                            ALU.subtract).then_inc(plo_set, 1)

            pairs(gp, step)
            gp.wait_ge(const_set, 1)
            for t in range(NT):
                gp.wait_ge(x1_set, t + 1)
                if t >= 2:
                    gp.wait_ge(y_set, t - 1)
                nc.gpsimd.tensor_tensor(x1b[:, t % 2, :], x1[:, t % 2, :], gbias[:], ALU.add).then_inc(x1b_set, 1)

        @block.scalar
        def _(act):
            def fold_g(p):
                wait(act, f1_done, p + 1)
                nc.scalar.activation(g_sb[:], ps_f[:, 0:P], ACT.Copy).then_inc(g_set, 1)

            def fold_mt(p):
                wait(act, f2_done, p + 1)
                nc.scalar.activation(mt_sb[:], ps_f[:, 0:DM], ACT.Copy).then_inc(mtsb_set, 1)

            def fold_m(p):
                wait(act, f3_done, p + 1)
                nc.scalar.activation(m_hi[:], ps_f[:, 0:DM].rearrange("p (c n) -> p c n", c=IC),
                                     ACT.Copy).then_inc(mhi_set, 1)

            def fold_n(p):
                wait(act, nf_done, p + 1)
                nc.scalar.activation(n_hi[:, p, :], ps_f[:, 0:DM], ACT.Copy).then_inc(nhi_set, 1)

            def queries_high(p, b):
                wait(act, q_done, 4 * p + b + 1)
                wait(act, st_done, 4 * p + b - 3)
                for h in range(2):
                    ins = nc.scalar.activation(q_hl[0:DC, b, h, :],
                                               ps_a[DC * h:DC * h + DC, 0:S], ACT.Copy)
                ins.then_inc(qhi_set, 1)

            def maxima_row(p, b):
                wait(act, mt_done, 4 * p + b + 1)
                nc.scalar.activation(mxt[:, b, :], ps_s[0:4, 0, 0:P], ACT.Copy).then_inc(mxt_set, 1)

            def exps(p, b):
                g = 4 * p + b
                scores_t = ps_t[:, b % 2, :, :].rearrange("p j n -> p (j n)")
                wait(act, st_done, g + 1)
                wait(act, plo_set, g - 1)
                nc.scalar.activation(p_f32[:, b % 2, :], scores_t, ACT.Exp).then_inc(p32_set, 1)
                if b == 1 and is_at_most(p, NP - 2):
                    fold_n(p + 1)
                if b == 2 and is_at_most(p, NP - 3):
                    fold_g(p + 2)
                if b == 3 and is_at_most(p, NP - 3):
                    fold_mt(p + 2)
                wait(act, pv_done, g - 3)
                nc.scalar.activation(p_hi[:, b].rearrange("p j h s -> p (j h s)"), scores_t,
                                     ACT.Exp).then_inc(phi_set, 1)

            def context_high(t):
                act.wait_ge(ctt_done, t + 1)
                if t >= 2:
                    act.wait_ge(o_done, t - 1)
                nc.scalar.activation(ct_hi[:, t % 2].rearrange("p a b -> p (a b)"),
                                     ps_ct(t), ACT.Copy).then_inc(cthi_set, 1)

            def deviation(i):
                act.wait_ge(var_set, i + 1)
                half = slice(i * NT // 2, (i + 1) * NT // 2)
                nc.scalar.activation(std[:, half], mv[:, half, 1], ACT.Sqrt, bias=eps[:, 0:1]).then_inc(std_set, 1)

            def turned_high(i):
                act.wait_ge(xt_done, i + 1)
                nc.scalar.activation(xt_hi[:, :, i * T // 2:(i + 1) * T // 2], ps_t[:, i], ACT.Copy).then_inc(xthi_set, 1)

            def keys_high(i):
                act.wait_ge(k_done, i + 1)
                nc.scalar.activation(k_hi[:, i * T // 2:(i + 1) * T // 2], ps_s[:, i, :], ACT.Copy).then_inc(khi_set, 1)

            act.wait_ge(eps_set, 1)
            nc.scalar.activation(warm[:], eps[:], ACT.Sqrt)
            fold_g(0)
            deviation(0)
            fold_mt(0)
            turned_high(0)
            fold_m(0)
            deviation(1)
            keys_high(0)
            queries_high(0, 0)
            keys_high(1)
            turned_high(1)
            queries_high(0, 1)
            act.wait_ge(gate_in, 16)
            nc.scalar.activation(tanhs[:], gate[:], ACT.Tanh).then_inc(tanh_set, 1)
            fold_g(1)
            maxima_row(0, 0)
            queries_high(0, 2)
            fold_mt(1)
            fold_n(0)
            act.wait_ge(vinv_set, 1)
            nc.scalar.activation(v_hi[:, :, 0:DC], ps_c[:].rearrange("p (t d) -> p t d", t=NT), ACT.Copy,
                                 scale=vscale[:, 0:1]).then_inc(vhi_set, 1)

            def step(p):
                for b in range(B):
                    if is_at_most(p, NP - 2) or b + 3 < B:
                        queries_high(p + (b + 3) // B, (b + 3) % B)
                    if b == 0 and is_at_most(p, NP - 2):
                        fold_m(p + 1)
                    if is_at_most(p, NP - 2) or b + 1 < B:
                        maxima_row(p + (b + 1) // B, (b + 1) % B)
                    if isinstance(p, int) and p == NP - 1 and b == B - 1:
                        context_high(0)
                    exps(p, b)

            pairs(act, step)

            def normed_copy(t):
                act.wait_ge(xt2_done, t + 1)
                if t >= 2:
                    act.wait_ge(ffn_done, t - 1)
                nc.scalar.activation(xt2[:, t % 2].rearrange("p c n -> p (c n)"), ps_x2, ACT.Copy).then_inc(xt2_set, 1)

            nc.scalar.activation(warm[:], eps[:], ACT.Sqrt)
            context_high(1)
            for t in range(NT):
                if t >= 1:
                    normed_copy(t - 1)
                act.wait_ge(var2_set, t + 1)
                nc.scalar.activation(sd2[:, t % 2:t % 2 + 1], mv2[:, t % 2, 1:2], ACT.Sqrt,
                                     bias=eps[:, 0:1]).then_inc(std2_set, 1)
                if t + 2 < NT:
                    context_high(t + 2)
            normed_copy(NT - 1)

        @block.vector
        def _(v):
            chain = [0]

            def link(ins):
                chain[0] += 1
                ins.then_inc(dve, 1)
                v.wait_ge(dve, chain[0])

            def split_low(out_, whole, high, done):
                nc.vector.tensor_tensor(out_, whole, high, ALU.subtract).then_inc(done, 1)

            def fold_m(p):
                wait(v, mhi_set, p + 1)
                split_low(m_lo[:], ps_f[:, 0:DM].rearrange("p (c n) -> p c n", c=IC), m_hi[:].bitcast(F32), mlo_set)

            def fold_n(p):
                wait(v, nhi_set, p + 1)
                split_low(n_lo[:, p, :], ps_f[:, 0:DM], n_hi[:, p, :].bitcast(F32), nlo_set)

            nc.vector.memset(eps[:], EPS).then_inc(eps_set, 1)
            nc.vector.memset(k_lo[DC:DC + 1, :].bitcast(F32), -1.0)
            nc.vector.memset(v_hi[:, :, DC:DC + 1], 1.0)

            def moments(i):
                tiles = range(i * NT // 2, (i + 1) * NT // 2)
                for t in tiles:
                    if t in (0, 2, 4):
                        v.wait_ge(x_in[t // 2], 16)
                    ins = nc.vector.bn_stats(stats[:, t, :], x_sb[:, t, :])
                link(ins)
                for t in tiles:
                    ins = nc.vector.bn_aggr(mv[:, t, :], stats[:, t, :])
                ins.then_inc(var_set, 1)

            def normalise(i):
                half = slice(i * NT // 2, (i + 1) * NT // 2)
                v.wait_ge(std_set, i + 1)
                link(nc.vector.reciprocal(rstd[:, half], std[:, half]))
                for t in range(i * NT // 2, (i + 1) * NT // 2):
                    nc.vector.tensor_scalar(xn[:, t, :], x_sb[:, t, :], mv[:, t, 0:1], rstd[:, t:t + 1],
                                            ALU.subtract, ALU.mult).then_inc(xn_set, 1)

            def turned_low(i):
                v.wait_ge(xthi_set, i + 1)
                rows = slice(i * T // 2, (i + 1) * T // 2)
                split_low(xt_lo[:, :, rows], ps_t[:, i], xt_hi[:, :, rows].bitcast(F32), xtlo_set)

            def keys_low(i):
                v.wait_ge(khi_set, i + 1)
                rows = slice(i * T // 2, (i + 1) * T // 2)
                split_low(k_lo[0:DC, rows], ps_s[0:DC, i, :], k_hi[0:DC, rows].bitcast(F32), klo_set)

            def queries_low(p, b):
                wait(v, qhi_set, 4 * p + b + 1)
                for h in range(2):
                    ins = nc.vector.tensor_tensor(q_hl[DC:P, b, h, :], ps_a[DC * h:DC * h + DC, 0:S],
                                                  q_hl[0:DC, b, h, :].bitcast(F32), ALU.subtract)
                ins.then_inc(qlo_set, 1)

            def maxima(p, b, h, nth):
                wait(v, s_done, 2 * (4 * p + b) + nth + 1)
                nc.vector.tensor_reduce(mx[:, b, 2 * h:2 * h + 2], ps_s[:, h, :].rearrange("p (c l) -> p c l", c=SC),
                                        AX_X, ALU.max).then_inc(max_set, 1)

            def context(p, b):
                g = 4 * p + b
                cs = ps_c[:, 0:4 * (DC + 1)].rearrange("p (n d) -> p n d", n=4)
                wait(v, pv_done, g + 1)
                nc.vector.reciprocal(rden[:, b, :], cs[:, :, DC]).then_inc(rec_set, 1)
                wait(v, rec_set, g + 1)
                nc.vector.tensor_tensor(cx[:, SC * b:SC * b + SC, p, :].rearrange("p c (h d) -> p h c d", h=2),
                                        cs[:, :, 0:DC].rearrange("p (h c) d -> p h c d", h=2),
                                        rden[:, b, :].rearrange("p (h c) -> p h c", h=2).unsqueeze(3)
                                        .broadcast_to([P, 2, SC, DC]), ALU.mult).then_inc(cx_set, 1)

            moments(0)
            normalise(0)
            moments(1)
            turned_low(0)
            fold_m(0)
            normalise(1)
            keys_low(0)
            queries_low(0, 0)
            keys_low(1)
            queries_low(0, 1)
            maxima(0, 0, 1, 0)
            maxima(0, 0, 0, 1)
            turned_low(1)
            v.wait_ge(v_done, 1)
            nc.vector.tensor_reduce(vmax[:], ps_c[:], AX_X, ALU.max,
                                    apply_absolute_value=True).then_inc(vmax_set, 1)
            queries_low(0, 2)
            maxima(0, 1, 1, 0)
            maxima(0, 1, 0, 1)
            v.wait_ge(vall_set, 1)
            link(nc.vector.tensor_scalar(vinv[:], vall[:], TINY, 1.0 / V_TOP, ALU.max, ALU.mult))
            nc.vector.reciprocal(vscale[:], vinv[:]).then_inc(vinv_set, 1)
            fold_n(0)
            v.wait_ge(vhi_set, 1)
            nc.vector.scalar_tensor_tensor(out=v_lo[:], in0=ps_c[:].rearrange("p (t d) -> p t d", t=NT),
                                           scalar=vscale[:, 0:1], in1=v_hi[:, :, 0:DC],
                                           op0=ALU.mult, op1=ALU.subtract).then_inc(v_set, 1)
            v.wait_ge(tanh_set, 1)
            nc.vector.tensor_tensor(ga[:], tanhs[:, 0:1], vinv[:], ALU.mult)

            def step(p):
                for b in range(B):
                    looks_2 = is_at_most(p, NP - 2) or b + 2 < B
                    looks_3 = is_at_most(p, NP - 2) or b + 3 < B
                    p2, b2 = p + (b + 2) // B, (b + 2) % B
                    if looks_2 and b > 0:
                        maxima(p2, b2, 1, 0)
                    if looks_3:
                        queries_low(p + (b + 3) // B, (b + 3) % B)
                    if b == 0 and is_at_most(p, NP - 2):
                        fold_m(p + 1)
                    if looks_2:
                        maxima(p2, b2, 0, 0 if b == 0 else 1)
                    if looks_2 and b == 0:
                        maxima(p2, b2, 1, 1)
                    if b == 1 and is_at_most(p, NP - 2):
                        fold_n(p + 1)
                    if b >= 2:
                        context(p, b - 2)
                    elif not isinstance(p, int) or p > 0:
                        context(p - 1, b + 2)

            pairs(v, step)
            def context_low(t):
                v.wait_ge(cthi_set, t + 1)
                if t >= 2:
                    v.wait_ge(o_done, t - 1)
                nc.vector.tensor_tensor(ct_lo[:, t % 2].rearrange("p a b -> p (a b)"),
                                        ps_ct(t),
                                        ct_hi[:, t % 2].rearrange("p a b -> p (a b)").bitcast(F32),
                                        ALU.subtract).then_inc(ctlo_set, 1)

            def residual(t):
                i = t % 2
                v.wait_ge(o_done, t + 1)
                nc.vector.scalar_tensor_tensor(out=x1[:, i, :], in0=ps_o(t), scalar=ga[:, 0:1], in1=x_sb[:, t, :],
                                               op0=ALU.mult, op1=ALU.add).then_inc(x1_set, 1)
                v.wait_ge(x1_set, t + 1)
                link(nc.vector.bn_stats(st2[:, i, :], x1[:, i, :]))
                nc.vector.bn_aggr(mv2[:, i, :], st2[:, i, :]).then_inc(var2_set, 1)
                v.wait_ge(std2_set, t + 1)
                link(nc.vector.reciprocal(rs2[:, i:i + 1], sd2[:, i:i + 1]))
                nc.vector.tensor_scalar(xn2[:, i, :], x1[:, i, :], mv2[:, i, 0:1], rs2[:, i:i + 1],
                                        ALU.subtract, ALU.mult).then_inc(xn2_set, 1)

            def result(t):
                v.wait_ge(ffn_done, t + 1)
                v.wait_ge(x1b_set, t + 1)
                if t >= 2:
                    v.wait_ge(y_out[t % 2], 16 * (t // 2))
                nc.vector.tensor_tensor(y[:, t % 2, :], ps_y, x1b[:, t % 2, :], ALU.add).then_inc(y_set, 1)

            context_low(0)
            context(NP - 1, B - 2)
            context_low(1)
            context(NP - 1, B - 1)
            for t in range(NT):
                residual(t)
                if t >= 1:
                    result(t - 1)
                if t + 2 < NT:
                    context_low(t + 2)
            result(NT - 1)

        @block.tensor
        def _(pe):
            def mm(o, lhsT, rhs, first, last):
                return nc.tensor.matmul(o, lhsT=lhsT, rhs=rhs, start=first, stop=last)

            def fold_1(p):
                wait(pe, f1w_in, 16 * (p + 1))
                kcq = f1w[:, 0:2 * 2 * K].rearrange("q (c h k) -> q c h k", c=2, h=2)
                wqr = f1w[:, 2 * 2 * K:].rearrange("q (c h r) -> q c h r", c=2, h=2)
                for h in range(2):
                    for c in range(2):
                        ins = mm(ps_f[:, R * h:R * h + R], kcq[:, c, h, :], wqr[:, c, h, :], c == 0, c == 1)
                ins.then_inc(f1_done, 1)

            def fold_2(p):
                wait(pe, g_set, p + 1)
                wait(pe, wq_in, 16 * (p + 1))
                for h in range(2):
                    ins = mm(ps_f[R * h:R * h + R, 0:DM], g_sb[:, R * h:R * h + R], wq[:, h, :], True, True)
                ins.then_inc(f2_done, 1)

            def fold_3(p):
                wait(pe, mtsb_set, p + 1)
                wait(pe, wkr_in, 16 * (p + 1))
                for c in range(IC):
                    ins = mm(ps_f[:, P * c:P * c + P], mt_sb[:, P * c:P * c + P], wkr[:], True, True)
                ins.then_inc(f3_done, 1)

            def fold_n(p):
                wait(pe, wo_in, 16 * (p + 1))
                for h in range(2):
                    ins = mm(ps_f[DC * h:DC * h + DC, 0:DM], wo[:, DC * h:DC * h + DC],
                             wo[:, 2 * DC + DM * h:2 * DC + DM * h + DM], True, True)
                ins.then_inc(nf_done, 1)

            def queries(p, b):
                wait(pe, mlo_set, p + 1)
                rows = slice(b * S, (b + 1) * S)
                n = 0
                for c in range(IC):
                    for w, xt in ((m_hi, xt_hi), (m_hi, xt_lo), (m_lo, xt_hi)):
                        ins = mm(ps_a[:, 0:S], w[:, c, :], xt[:, c, rows], n == 0, n == 3 * IC - 1)
                        n += 1
                ins.then_inc(q_done, 1)

            def scores(p, b, h):
                e = 4 * p + b
                wait(pe, qlo_set, e + 1)
                if h == 0:
                    wait(pe, mxt_set, e)
                else:
                    wait(pe, max_set, 2 * e)
                for c in range(SC):
                    ins = mm(ps_s[:, h, S * c:S * c + S], q_hl[:, b, h, P * c:P * c + P],
                             k_hi[:, b * S:(b + 1) * S], True, True)
                ins.then_inc(s_done, 1)

            def scores_t(p, b):
                g = 4 * p + b
                wait(pe, qhm_in[b], 16 * (p + 1))
                wait(pe, mrow_in[b], 16 * (p + 1))
                wait(pe, phi_set, g - 1)
                for j in range(SC):
                    keys = slice(b * S + P * j, b * S + P * j + P)
                    o = ps_t[:, b % 2, j, :]
                    mm(o, k_hi[:, keys], q_hl[:, b].rearrange("k h s -> k (h s)"), True, False)
                    ins = mm(o, k_lo[:, keys], q_hm[:, b].rearrange("k h s -> k (h s)"), False, True)
                ins.then_inc(st_done, 1)

            def turn_maxima(p, b):
                wait(pe, max_set, 2 * (4 * p + b) + 2)
                nc.tensor.transpose(ps_s[0:4, 0, 0:P], mx[:, b, :], ident).then_inc(mt_done, 1)

            def values(p, b):
                g = 4 * p + b
                wait(pe, plo_set, g + 1)
                wait(pe, cx_set, g)
                for h in range(2):
                    for c in range(SC):
                        at = (2 * h + c) * (DC + 1)
                        for j in range(SC):
                            ph = p_hi[:, b, j, h, P * c:P * c + P]
                            pl = p_lo[:, b, j, h, P * c:P * c + P]
                            vh, vl = v_hi[:, SC * b + j, :], v_lo[:, SC * b + j, :]
                            mm(ps_c[:, at:at + DC + 1], ph, vh, j == 0, False)
                            mm(ps_c[:, at:at + DC], ph, vl, False, False)
                            ins = mm(ps_c[:, at:at + DC + 1], pl, vh, False, j == SC - 1)
                ins.then_inc(pv_done, 1)

            def turn_context(t):
                if t >= 2:
                    pe.wait_ge(ctlo_set, t - 1)
                pe.wait_ge(cx_set, STEPS - B + t // SC + 1)
                for p in range(NP):
                    ins = nc.tensor.transpose(ps_ct(t)[:, P * p:P * p + P], cx[:, t, p, :], ident)
                ins.then_inc(ctt_done, 1)

            def turn_rows(i):
                for t in range(NT // 2):
                    pe.wait_ge(xn_set, i * NT // 2 + t + 1)
                    for c in range(IC):
                        ins = nc.tensor.transpose(ps_t[:, i, c, P * t:P * t + P],
                                                  xn[:, i * NT // 2 + t, P * c:P * c + P], ident)
                ins.then_inc(xt_done, 1)

            def keys(i):
                pe.wait_ge(turned_set, i + 1)
                mm(ps_s[:, i, :], ident4, turned[:, i * T // 2:(i + 1) * T // 2], True, True).then_inc(k_done, 1)

            fold_1(0)
            fold_2(0)
            pe.wait_ge(ident_in, 16)
            turn_rows(0)
            fold_3(0)
            keys(0)
            pe.wait_ge(xtlo_set, 1)
            queries(0, 0)
            keys(1)
            turn_rows(1)
            pe.wait_ge(qlo_set, 1)
            queries(0, 1)
            pe.wait_ge(klo_set, 2)
            scores(0, 0, 1)
            scores(0, 0, 0)
            for t in range(NT):
                ins = mm(ps_c[:, DC * t:DC * t + DC], turned[:, P * t:P * t + P], ident4[:, 0:DC], True, True)
            ins.then_inc(v_done, 1)
            pe.wait_ge(max_set, 1)
            fold_1(1)
            turn_maxima(0, 0)
            pe.wait_ge(qlo_set, 2)
            pe.wait_ge(xtlo_set, 2)
            queries(0, 2)
            fold_2(1)
            pe.wait_ge(mtsb_set, 2)
            scores(0, 1, 1)
            scores(0, 1, 0)
            pe.wait_ge(max_set, 3)
            fold_n(0)

            def step(p):
                for b in range(B):
                    looks_1 = is_at_most(p, NP - 2) or b + 1 < B
                    looks_2 = is_at_most(p, NP - 2) or b + 2 < B
                    p1, b1 = p + (b + 1) // B, (b + 1) % B
                    p2, b2 = p + (b + 2) // B, (b + 2) % B
                    if is_at_most(p, NP - 2) or b + 3 < B:
                        wait(pe, qlo_set, 4 * p + b + 3)
                        queries(p + (b + 3) // B, (b + 3) % B)
                    if b == 0 and is_at_most(p, NP - 2):
                        wait(pe, max_set, 2 * (4 * p + 2))
                        if isinstance(p, int) and p == 0:
                            pe.wait_ge(nlo_set, 1)
                        fold_3(p + 1)
                    if looks_1:
                        turn_maxima(p1, b1)
                    if b > 0 and looks_2:
                        if b == 2:
                            wait(pe, nlo_set, p + 2)
                        if b == 3 and is_at_most(p, NP - 3):
                            wait(pe, g_set, p + 3)
                        scores(p2, b2, 1)
                    if isinstance(p, int) and p == NP - 1 and b == B - 1:
                        pe.wait_ge(mxt_set, STEPS)
                        turn_context(0)
                    scores_t(p, b)
                    if looks_2:
                        scores(p2, b2, 0)
                    if b == 0:
                        if is_at_most(p, NP - 2):
                            wait(pe, mlo_set, p + 2)
                        scores(p2, b2, 1)
                    elif is_at_most(p, NP - 2 if b == 1 else NP - 3):
                        wait(pe, max_set, 2 * (4 * p + b + 2) + 1)
                        (None, fold_n, fold_1, fold_2)[b](p + 1 if b == 1 else p + 2)
                    if isinstance(p, int) and p == 0 and b == 2:
                        pe.wait_ge(v_set, 1)
                    if b >= 2:
                        values(p, b - 2)
                    elif not isinstance(p, int) or p > 0:
                        values(p - 1, b + 2)

            pairs(pe, step)
            def project(t):
                pe.wait_ge(ctlo_set, t + 1)
                if t >= 2:
                    pe.wait_ge(x1_set, t - 1)
                n = 0
                for p in range(NP):
                    for c, w in ((ct_hi, n_hi), (ct_hi, n_lo), (ct_lo, n_hi)):
                        ins = mm(ps_o(t), c[:, t % 2, p, :], w[:, p, :], n == 0, n == 3 * NP - 1)
                        n += 1
                ins.then_inc(o_done, 1)

            def linear(t):
                pe.wait_ge(xn2_set, t + 1)
                if t >= 1:
                    pe.wait_ge(xt2_set, t)
                for c in range(IC):
                    ins = nc.tensor.transpose(ps_x2[:, P * c:P * c + P], xn2[:, t % 2, P * c:P * c + P], ident)
                ins.then_inc(xt2_done, 1)

            def linear_mm(t):
                pe.wait_ge(xt2_set, t + 1)
                if t >= 1:
                    pe.wait_ge(y_set, t)
                for c in range(IC):
                    ins = mm(ps_y, xt2[:, t % 2, c, :], wffn[:, c, :], c == 0, c == IC - 1)
                ins.then_inc(ffn_done, 1)

            pe.wait_ge(phi_set, STEPS - 1)
            turn_context(1)
            values(NP - 1, B - 2)
            project(0)
            values(NP - 1, B - 1)
            turn_context(2)
            pe.wait_ge(cx_set, STEPS)
            pe.wait_ge(const_set, 1)
            project(1)
            for t in range(1, NT):
                linear(t - 1)
                if t + 2 < NT:
                    turn_context(t + 2)
                linear_mm(t - 1)
                if t + 1 < NT:
                    project(t + 1)
            linear(NT - 1)
            linear_mm(NT - 1)


def _rope():
    import numpy as np
    inv = (1.0 / np.power(np.float32(10000.0), np.arange(0, DC, 2, dtype=np.float32) / np.float32(DC))).astype(np.float32)
    f = (np.arange(S, dtype=np.float32)[:, None] * inv[None, :]).astype(np.float32).astype(np.float64)
    sin, cos = np.repeat(np.sin(f), 2, -1), np.repeat(np.cos(f), 2, -1)
    sin[:, :DC // 2] *= -1.0
    return np.stack([cos, sin]).astype(np.float32)


def kernel(x, ctx_512, g_xattn, g_ffn, L0_xattn_Wq, L0_xattn_w_kc_q, L0_xattn_w_kc_kv, L0_xattn_W_qr,
           L0_xattn_W_kr, L0_xattn_Wo, L0_ffn_weight, L0_ffn_scale_weight, L0_ffn_bias):
    import numpy as np
    import concourse.bacc as bacc
    from concourse.bass_utils import run_bass_kernel_spmd

    A = lambda a: np.ascontiguousarray(np.asarray(a))
    kv = A(ctx_512)
    swapped = np.concatenate([kv[..., DC // 2:], kv[..., :DC // 2]], -1)
    both = np.stack([kv, swapped]).reshape(2, T, DC)
    rope = _rope()
    Wq, kcq, kckv = A(L0_xattn_Wq), A(L0_xattn_w_kc_q), A(L0_xattn_w_kc_kv)
    Wqr, Wkr, Wo = A(L0_xattn_W_qr), A(L0_xattn_W_kr), A(L0_xattn_Wo)
    kcq_t = kcq.reshape(NP, 2, K, 2, QC).transpose(0, 4, 3, 1, 2).reshape(NP, QC, 4 * K)
    wqr_t = Wqr.reshape(NP, 2, 2, QC, R).transpose(0, 3, 2, 1, 4).reshape(NP, QC, 4 * R)
    wkr_bd = np.zeros((NP, 2, R, 2, DC), np.float32)
    for h in range(2):
        wkr_bd[:, h, :, h, :] = Wkr.reshape(NP, 2, DC, R)[:, h].transpose(0, 2, 1)
    kckv_t = kckv.reshape(NP, 2, K, DC).transpose(0, 2, 1, 3).reshape(NP, K, 2 * DC)
    wo_t = Wo.T.reshape(NP, 2, K, DM).transpose(0, 2, 1, 3).reshape(NP, K, 2 * DM)
    arrays = {
        "x_rows": A(x).reshape(NT, P, DM),
        "kv_rope": np.concatenate([both.transpose(0, 2, 1), rope.transpose(0, 2, 1)], -1).reshape(P, T + S),
        "identities": np.stack([np.eye(P), np.tile(np.eye(DC), (2, 2))], 1).astype(np.float32),
        "w_f1": np.concatenate([kcq_t, wqr_t], -1),
        "w_q": Wq.reshape(NP, 2, K, DM).transpose(0, 2, 1, 3),
        "w_kr": wkr_bd.reshape(NP, P, P),
        "w_o": np.concatenate([kckv_t, wo_t], -1),
        "w_ffn": A(L0_ffn_weight).T.reshape(IC, P, DM).transpose(1, 0, 2),
        "rows_o": np.stack([A(L0_ffn_scale_weight), A(L0_ffn_bias)]),
        "gates": np.concatenate([A(g_xattn).reshape(1), A(g_ffn).reshape(1)]),
    }
    arrays = {f"{n}_dram": np.ascontiguousarray(a) for n, a in arrays.items()}
    nc = bacc.Bacc("TRN2", target_bir_lowering=False, num_devices=1)
    aps = [nc.dram_tensor(n, a.shape, mybir.dt.from_np(a.dtype), kind="ExternalInput").ap() for n, a in arrays.items()]
    aps[0] = aps[0].rearrange("t p n -> p t n")
    out = nc.dram_tensor("out_dram", (NT, P, DM), F32, kind="ExternalOutput").ap()
    flamingo_kernel(nc, *aps, out.rearrange("t p n -> p t n"))
    r = run_bass_kernel_spmd(nc, [arrays], core_ids=[0])
    return r.results[0]["out_dram"].reshape(B, S, DM)
```

```python
from contextlib import ExitStack

import concourse.bass as bass
from concourse import mybir

P = 128
F32 = mybir.dt.float32
F32R = mybir.dt.float32r
F16 = mybir.dt.float16
ACT = mybir.ActivationFunctionType
ALU = mybir.AluOpType
AX_X = mybir.AxisListType.X
RMAX = bass.bass_isa.ReduceOp.max

B, S, DM = 4, 256, 256
H, K, DC, DQ, R = 16, 128, 64, 192, 64
T = B * S
NT = T // P
NP = H // 2
STEPS = NP * B
IC = DM // P
SC = S // P
QC = 96
EPS = 1e-5
V_TOP = 1024.0
TINY = 1e-20


def flamingo_kernel(nc, x, kv_rope, identities, w_f1, w_q, w_kr, w_o,
                    w_ffn, rows_o, gates, out):
    ctx = ExitStack()
    with ctx:
        def sb(name, shape, dt=F32):
            return ctx.enter_context(nc.sbuf_tensor(name, shape, dt))

        def pb(name, shape):
            return ctx.enter_context(nc.psum_tensor(name, shape, F32))

        def sem(name):
            return ctx.enter_context(nc.semaphore(name))

        x_sb = sb("x_sb", [P, NT, DM])
        kvr = sb("kvr", [P, T + S])
        idents = sb("idents", [P, 2, P])
        f1w = sb("f1w", [QC, 2 * 2 * K + 2 * 2 * R])
        wq = sb("wq", [P, 2, DM])
        wkr = sb("wkr", [P, P])
        wo = sb("wo", [P, 2 * DC + 2 * DM])
        ffn_raw = sb("ffn_raw", [P, IC, DM])
        rowo = sb("rowo", [P, 2, DM])
        gate = sb("gate", [P, 2])
        stats = sb("stats", [P, NT, 6])
        mv = sb("mv", [P, NT, 2])
        std = sb("std", [P, NT])
        rstd = sb("rstd", [P, NT])
        offset = sb("offset", [P, NT])
        eps = sb("eps", [P, 1])
        warm = sb("warm", [P, 1])
        xn = sb("xn", [P, NT, DM])
        xt_hi = sb("xt_hi", [P, IC, T], F32R)
        xt_lo = sb("xt_lo", [P, IC, T], F32R)
        turned = sb("turned", [P, T])
        k_hi = sb("k_hi", [P, T], F32R)
        k_lo = sb("k_lo", [DC + 1, T], F32R)
        v_hi = sb("v_hi", [P, NT, DC + 1], F16)
        v_lo = sb("v_lo", [P, NT, DC], F16)
        vmax = sb("vmax", [P, 1])
        vall = sb("vall", [P, 1])
        vinv = sb("vinv", [P, 1])
        vscale = sb("vscale", [P, 1])
        tanhs = sb("tanhs", [P, 2])
        ga = sb("ga", [P, 1])
        wffn = sb("wffn", [P, IC, DM])
        wffn_hi = sb("wffn_hi", [P, IC, DM], F32R)
        wffn_lo = sb("wffn_lo", [P, IC, DM], F32R)
        gbias = sb("gbias", [P, DM])
        g_sb = sb("g_sb", [P, P])
        mt_sb = sb("mt_sb", [P, DM])
        m_hi = sb("m_hi", [P, IC, P], F32R)
        m_lo = sb("m_lo", [P, IC, P], F32R)
        n_hi = sb("n_hi", [P, NP, DM], F32R)
        n_lo = sb("n_lo", [P, NP, DM], F32R)
        q_hl = sb("q_hl", [P, B, 2, S], F32R)
        q_hm = sb("q_hm", [DC + 1, B, 2, S], F32R)
        mx = sb("mx", [P, B, 4])
        mxt = sb("mxt", [4, B, P], F32R)
        p_f32 = sb("p_f32", [P, 2, 4 * S])
        p_hi = sb("p_hi", [P, B, SC, 2, S], F16)
        p_lo = sb("p_lo", [P, B, SC, 2, S], F16)
        rden = sb("rden", [P, B, 4])
        cx = sb("cx", [P, NT, NP, P])
        ct_hi = sb("ct_hi", [P, 2, NP, P], F32R)
        ct_lo = sb("ct_lo", [P, 2, NP, P], F32R)
        x1 = sb("x1", [P, 2, DM])
        x1b = sb("x1b", [P, 2, DM])
        xn2 = sb("xn2", [P, 2, DM])
        st2 = sb("st2", [P, 2, 6])
        mv2 = sb("mv2", [P, 2, 2])
        sd2 = sb("sd2", [P, 2])
        rs2 = sb("rs2", [P, 2])
        xt2_hi = sb("xt2_hi", [P, 2, IC, P], F32R)
        xt2_lo = sb("xt2_lo", [P, 2, IC, P], F32R)
        y = sb("y", [P, NT, DM])

        ps_s = pb("ps_s", [P, 2, 512])
        ps_t = pb("ps_t", [P, 2, SC, 512])
        ps_c = pb("ps_c", [P, 512])
        ps_a = pb("ps_a", [P, 512])
        ps_f = ps_s[:, 1, :]
        ident, ident4 = idents[:, 0, :], idents[:, 1, :]

        def ps_o(t):
            return (ps_c if t > 0 and t % 2 == 0 else ps_a)[:, 0:DM]

        def ps_ct(t):
            return (ps_t[:, 0] if t % 2 else ps_s[:]).rearrange("p j n -> p (j n)")

        ps_x2 = ps_t[:, 1, 0, 0:DM]

        def ps_y(t):
            return ps_s[:, 0, 0:DM] if t == NT - 2 else ps_t[:, 1, 1, 0:DM]

        x_in = [sem(f"x_in{i}") for i in range(3)]
        kvr_in, ident_in, gate_in = sem("kvr_in"), sem("ident_in"), sem("gate_in")
        f1w_in, wq_in, wkr_in, wo_in = sem("f1w_in"), sem("wq_in"), sem("wkr_in"), sem("wo_in")
        ffn_in, small_in = sem("ffn_in"), sem("small_in")
        qhm_in = [sem(f"qhm_in{b}") for b in range(B)]
        mrow_in = [sem(f"mrow_in{b}") for b in range(B)]
        y_out = sem("y_out")
        xt_done, f1_done, f2_done, f3_done, nf_done, k_done, v_done = (sem(n) for n in (
            "xt_done", "f1_done", "f2_done", "f3_done", "nf_done", "k_done", "v_done"))
        q_done, s_done, st_done, mt_done, pv_done = (sem(n) for n in (
            "q_done", "s_done", "st_done", "mt_done", "pv_done"))
        ctt_done, o_done, xt2_done, ffn_done = (sem(n) for n in (
            "ctt_done", "o_done", "xt2_done", "ffn_done"))
        xthi_set, khi_set, g_set, mtsb_set, mhi_set, nhi_set = (sem(n) for n in (
            "xthi_set", "khi_set", "g_set", "mtsb_set", "mhi_set", "nhi_set"))
        qhi_set, p32_set, phi_set, mxt_set = (sem(n) for n in ("qhi_set", "p32_set", "phi_set", "mxt_set"))
        std_set, std2_set, xna_set = sem("std_set"), sem("std2_set"), sem("xna_set")
        tanh_set, vhi_set, cthi_set, xt2hi_set, whi_set = (sem(n) for n in (
            "tanh_set", "vhi_set", "cthi_set", "xt2hi_set", "whi_set"))
        dve = sem("dve")
        xn_set, xtlo_set, klo_set, vinv_set, v_set, mlo_set, nlo_set = (sem(n) for n in (
            "xn_set", "xtlo_set", "klo_set", "vinv_set", "v_set", "mlo_set", "nlo_set"))
        max_set, qlo_set, plo_set, cx_set = (sem(n) for n in ("max_set", "qlo_set", "plo_set", "cx_set"))
        vmax_set, const_set, ctlo_set, x1_set, xn2_set, y_set = (sem(n) for n in (
            "vmax_set", "const_set", "ctlo_set", "x1_set", "xn2_set", "y_set"))
        xt2lo_set, wlo_set = sem("xt2lo_set"), sem("wlo_set")
        rec_set, var_set, var2_set, eps_set, offset_set = (sem(n) for n in (
            "rec_set", "var_set", "var2_set", "eps_set", "offset_set"))
        st2_set = sem("st2_set")
        scaled_set, turned_set, vall_set, x1b_set = (sem(n) for n in (
            "scaled_set", "turned_set", "vall_set", "x1b_set"))

        def wait(eng, s, n):
            if not isinstance(n, int) or n > 0:
                eng.wait_ge(s, n)

        def pairs(eng, step):
            step(0)
            with eng.Fori(1, NP - 2) as p:
                step(p)
            step(NP - 2)
            step(NP - 1)

        def is_at_most(p, last):
            return p <= last if isinstance(p, int) else True

        def ps_b(b):
            return ps_t[:, b // 2, b % 2, :]

        LN_GROUPS = (range(0, 2), range(2, 4), range(4, NT))

        def rows_first(p, b):
            return b != 1 and is_at_most(p, NP - 3 if b == 3 else NP - 2)

        block = ctx.enter_context(nc.Block())

        @block.sync
        def _(sp):
            def load(buf, src, landed):
                sp.dma_start(buf, src).then_inc(landed, 16)

            load(x_sb[:, 0:2, :], x[:, 0:2, :], x_in[0])
            load(f1w[:], w_f1[0], f1w_in)
            load(x_sb[:, 2:4, :], x[:, 2:4, :], x_in[1])
            load(wq[:], w_q[0], wq_in)
            load(idents[:], identities, ident_in)
            load(wkr[:], w_kr[0], wkr_in)
            load(kvr[:], kv_rope, kvr_in)
            load(x_sb[:, 4:, :], x[:, 4:, :], x_in[2])
            load(gate[:], gates.partition_broadcast(P), gate_in)
            load(wo[:], w_o[0], wo_in)

            def copy_queries(e_pair, b):
                wait(sp, qhi_set, 4 * e_pair + b + 1)
                sp.dma_start(q_hm[0:DC, b].bitcast(F32), q_hl[0:DC, b].bitcast(F32)).then_inc(qhm_in[b], 16)

            def put_maxima(e_pair, b):
                wait(sp, mxt_set, 4 * e_pair + b + 1)
                sp.dma_start(q_hm[DC:DC + 1, b].bitcast(F32).rearrange("o h (c s) -> o (h c) s", c=SC),
                             mxt[:, b, :].bitcast(F32)).then_inc(mrow_in[b], 16)

            def reload(buf, src, used, n, landed):
                wait(sp, used, n)
                load(buf, src, landed)

            reload(f1w[:], w_f1[1], f1_done, 1, f1w_in)
            reload(wq[:], w_q[1], f2_done, 1, wq_in)
            reload(wkr[:], w_kr[1], f3_done, 1, wkr_in)
            load(ffn_raw[:], w_ffn, ffn_in)
            load(rowo[:], rows_o.partition_broadcast(P), small_in)
            copy_queries(0, 0)
            reload(f1w[:], w_f1[2], f1_done, 2, f1w_in)
            copy_queries(0, 1)
            put_maxima(0, 0)
            reload(wq[:], w_q[2], f2_done, 2, wq_in)
            copy_queries(0, 2)

            def step(p):
                for b in range(B):
                    looks_1 = is_at_most(p, NP - 2) or b + 1 < B
                    if looks_1:
                        put_maxima(p + (b + 1) // B, (b + 1) % B)
                    if is_at_most(p, NP - 2) or b + 3 < B:
                        copy_queries(p + (b + 3) // B, (b + 3) % B)
                    if b == 0 and is_at_most(p, NP - 3):
                        reload(wkr[:], w_kr[p + 2], f3_done, p + 2, wkr_in)
                    if b == 1 and is_at_most(p, NP - 2):
                        reload(wo[:], w_o[p + 1], nf_done, p + 1, wo_in)
                    if b == 2 and is_at_most(p, NP - 4):
                        reload(f1w[:], w_f1[p + 3], f1_done, p + 3, f1w_in)
                    if b == 3 and is_at_most(p, NP - 4):
                        reload(wq[:], w_q[p + 3], f2_done, p + 3, wq_in)

            step(0)
            with sp.Fori(1, NP - 3) as p:
                step(p)
            step(NP - 3)
            step(NP - 2)
            step(NP - 1)

            for t in range(NT):
                sp.wait_ge(y_set, t + 1)
                sp.dma_start(out[:, t, :], y[:, t, :]).then_inc(y_out, 16)
            sp.wait_ge(y_out, 16 * NT)

        @block.gpsimd
        def _(gp):
            gp.wait_ge(kvr_in, 16)
            for b in range(B):
                nc.gpsimd.tensor_tensor(turned[:, b * S:(b + 1) * S], kvr[:, b * S:(b + 1) * S], kvr[:, T:],
                                        ALU.mult).then_inc(turned_set, 1)
            gp.wait_ge(ffn_in, 16)
            gp.wait_ge(small_in, 16)
            nc.gpsimd.tensor_tensor(wffn[:], ffn_raw[:], rowo[:, 0, :].unsqueeze(1).broadcast_to([P, IC, DM]),
                                    ALU.mult).then_inc(scaled_set, 1)
            gp.wait_ge(vmax_set, 1)
            nc.gpsimd.partition_all_reduce(vall[:], vmax[:], P, RMAX).then_inc(vall_set, 1)

            def step(p):
                for b in range(B):
                    g = 4 * p + b
                    wait(gp, phi_set, g + 1)
                    wait(gp, pv_done, g - 3)
                    nc.gpsimd.tensor_tensor(p_lo[:, b].rearrange("p j h s -> p (j h s)"), p_f32[:, b % 2, :],
                                            p_hi[:, b].rearrange("p j h s -> p (j h s)"),
                                            ALU.subtract).then_inc(plo_set, 1)

            pairs(gp, step)
            gp.wait_ge(const_set, 1)
            for t in range(NT):
                gp.wait_ge(x1_set, t + 1)
                if t >= 2:
                    gp.wait_ge(y_set, t - 1)
                nc.gpsimd.tensor_tensor(x1b[:, t % 2, :], x1[:, t % 2, :], gbias[:], ALU.add).then_inc(x1b_set, 1)

        @block.scalar
        def _(act):
            def fold_g(p):
                wait(act, f1_done, p + 1)
                nc.scalar.activation(g_sb[:], ps_f[:, 0:P], ACT.Copy).then_inc(g_set, 1)

            def fold_mt(p):
                wait(act, f2_done, p + 1)
                nc.scalar.activation(mt_sb[:], ps_f[:, 0:DM], ACT.Copy).then_inc(mtsb_set, 1)

            def fold_m(p):
                wait(act, f3_done, p + 1)
                nc.scalar.activation(m_hi[:], ps_f[:, 0:DM].rearrange("p (c n) -> p c n", c=IC),
                                     ACT.Copy).then_inc(mhi_set, 1)

            def fold_n(p):
                wait(act, nf_done, p + 1)
                nc.scalar.activation(n_hi[:, p, :], ps_f[:, 0:DM], ACT.Copy).then_inc(nhi_set, 1)

            def queries_high(p, b):
                wait(act, q_done, 4 * p + b + 1)
                wait(act, st_done, 4 * p + b - 3)
                for h in range(2):
                    ins = nc.scalar.activation(q_hl[0:DC, b, h, :],
                                               ps_a[DC * h:DC * h + DC, 0:S], ACT.Copy)
                ins.then_inc(qhi_set, 1)

            def maxima_row(p, b):
                wait(act, mt_done, 4 * p + b + 1)
                nc.scalar.activation(mxt[:, b, :], ps_s[0:4, 0, 0:P], ACT.Copy).then_inc(mxt_set, 1)

            def exps(p, b):
                g = 4 * p + b
                scores_t = ps_t[:, b % 2, :, :].rearrange("p j n -> p (j n)")
                wait(act, st_done, g + 1)
                wait(act, plo_set, g - 1)
                nc.scalar.activation(p_f32[:, b % 2, :], scores_t, ACT.Exp).then_inc(p32_set, 1)
                if b == 1:
                    fold_n(p)
                if b == 2 and is_at_most(p, NP - 3):
                    fold_g(p + 2)
                if b == 3 and is_at_most(p, NP - 3):
                    fold_mt(p + 2)
                if isinstance(p, int) and p == NP - 1 and b + 2 < B:
                    maxima_row(p, b + 2)
                wait(act, pv_done, g - 3)
                nc.scalar.activation(p_hi[:, b].rearrange("p j h s -> p (j h s)"), scores_t,
                                     ACT.Exp).then_inc(phi_set, 1)

            def context_high(t):
                act.wait_ge(ctt_done, t + 1)
                if t >= 2:
                    act.wait_ge(o_done, t - 1)
                nc.scalar.activation(ct_hi[:, t % 2].rearrange("p a b -> p (a b)"),
                                     ps_ct(t), ACT.Copy).then_inc(cthi_set, 1)

            def deviation(i):
                act.wait_ge(var_set, i + 1)
                group = slice(LN_GROUPS[i].start, LN_GROUPS[i].stop)
                nc.scalar.activation(std[:, group], mv[:, group, 1], ACT.Sqrt, bias=eps[:, 0:1]).then_inc(std_set, 1)

            def normalise(t):
                act.wait_ge(offset_set, 1)
                nc.scalar.activation(xn[:, t, :], x_sb[:, t, :], ACT.Identity, bias=offset[:, t:t + 1],
                                     scale=rstd[:, t:t + 1]).then_inc(xna_set, 1)

            def turned_high(b):
                act.wait_ge(xt_done, b + 1)
                nc.scalar.activation(xt_hi[:, :, b * S:(b + 1) * S], ps_b(b).rearrange("p (c n) -> p c n", c=IC),
                                     ACT.Copy).then_inc(xthi_set, 1)

            def keys_high(b):
                act.wait_ge(k_done, b + 1)
                nc.scalar.activation(k_hi[:, b * S:(b + 1) * S], ps_b(b)[:, 0:S], ACT.Copy).then_inc(khi_set, 1)

            act.wait_ge(eps_set, 1)
            nc.scalar.activation(warm[:], eps[:], ACT.Sqrt)
            deviation(0)
            fold_g(0)
            deviation(1)
            turned_high(0)
            fold_mt(0)
            turned_high(1)
            fold_m(0)
            keys_high(0)
            queries_high(0, 0)
            deviation(2)
            keys_high(1)
            fold_g(1)
            normalise(4)
            normalise(5)
            queries_high(0, 1)
            normalise(6)
            normalise(7)
            turned_high(2)
            turned_high(3)
            fold_mt(1)
            maxima_row(0, 0)
            queries_high(0, 2)
            act.wait_ge(gate_in, 16)
            nc.scalar.activation(tanhs[:], gate[:], ACT.Tanh).then_inc(tanh_set, 1)
            keys_high(2)
            keys_high(3)

            def step(p):
                for b in range(B):
                    looks_1 = is_at_most(p, NP - 2) or b + 1 < B
                    if looks_1 and not (isinstance(p, int) and p == NP - 1 and b >= 1):
                        maxima_row(p + (b + 1) // B, (b + 1) % B)
                    if is_at_most(p, NP - 2) or b + 3 < B:
                        queries_high(p + (b + 3) // B, (b + 3) % B)
                    if b == 0 and is_at_most(p, NP - 2):
                        fold_m(p + 1)
                    if isinstance(p, int) and p == 0 and b == 0:
                        act.wait_ge(vinv_set, 1)
                        nc.scalar.activation(v_hi[:, :, 0:DC], ps_c[:].rearrange("p (t d) -> p t d", t=NT),
                                             ACT.Copy, scale=vscale[:, 0:1]).then_inc(vhi_set, 1)
                    if isinstance(p, int) and p == NP - 1 and b == B - 1:
                        context_high(0)
                    exps(p, b)
                    if isinstance(p, int) and p == NP - 2 and b == 2:
                        act.wait_ge(tanh_set, 1)
                        act.wait_ge(scaled_set, 1)
                        nc.scalar.activation(wffn_hi[:], wffn[:], ACT.Copy, scale=tanhs[:, 1:2]).then_inc(whi_set, 1)

            pairs(act, step)

            def normed_copy(t):
                act.wait_ge(xt2_done, t + 1)
                if t >= 2:
                    act.wait_ge(ffn_done, t - 1)
                nc.scalar.activation(xt2_hi[:, t % 2].rearrange("p c n -> p (c n)"), ps_x2, ACT.Copy).then_inc(xt2hi_set, 1)

            nc.scalar.activation(warm[:], eps[:], ACT.Sqrt)
            context_high(1)
            nc.scalar.activation(gbias[:], rowo[:, 1, :], ACT.Copy, scale=tanhs[:, 1:2]).then_inc(const_set, 1)
            for t in range(NT):
                if t >= 1:
                    normed_copy(t - 1)
                act.wait_ge(var2_set, t + 1)
                nc.scalar.activation(sd2[:, t % 2:t % 2 + 1], mv2[:, t % 2, 1:2], ACT.Sqrt,
                                     bias=eps[:, 0:1]).then_inc(std2_set, 1)
                if t + 2 < NT:
                    context_high(t + 2)
            normed_copy(NT - 1)

        @block.vector
        def _(v):
            chain = [0]

            def link(ins):
                chain[0] += 1
                ins.then_inc(dve, 1)
                v.wait_ge(dve, chain[0])

            def split_low(out_, whole, high, done):
                nc.vector.tensor_tensor(out_, whole, high, ALU.subtract).then_inc(done, 1)

            def fold_m(p):
                wait(v, mhi_set, p + 1)
                split_low(m_lo[:], ps_f[:, 0:DM].rearrange("p (c n) -> p c n", c=IC), m_hi[:].bitcast(F32), mlo_set)

            def fold_n(p):
                wait(v, nhi_set, p + 1)
                split_low(n_lo[:, p, :], ps_f[:, 0:DM], n_hi[:, p, :].bitcast(F32), nlo_set)

            nc.vector.memset(eps[:], EPS).then_inc(eps_set, 1)
            nc.vector.memset(k_lo[DC:DC + 1, :].bitcast(F32), -1.0)
            nc.vector.memset(v_hi[:, :, DC:DC + 1], 1.0)

            def moments(i):
                v.wait_ge(x_in[i], 16)
                for t in LN_GROUPS[i]:
                    ins = nc.vector.bn_stats(stats[:, t, :], x_sb[:, t, :])
                link(ins)
                for t in LN_GROUPS[i]:
                    ins = nc.vector.bn_aggr(mv[:, t, :], stats[:, t, :])
                ins.then_inc(var_set, 1)

            def normalise(i):
                v.wait_ge(std_set, i + 1)
                group = slice(LN_GROUPS[i].start, LN_GROUPS[i].stop)
                link(nc.vector.reciprocal(rstd[:, group], std[:, group]))
                for t in LN_GROUPS[i]:
                    nc.vector.tensor_scalar(xn[:, t, :], x_sb[:, t, :], mv[:, t, 0:1], rstd[:, t:t + 1],
                                            ALU.subtract, ALU.mult).then_inc(xn_set, 1)

            def turned_low(b):
                v.wait_ge(xthi_set, b + 1)
                rows = slice(b * S, (b + 1) * S)
                split_low(xt_lo[:, :, rows], ps_b(b).rearrange("p (c n) -> p c n", c=IC),
                          xt_hi[:, :, rows].bitcast(F32), xtlo_set)

            def keys_low(b):
                v.wait_ge(khi_set, b + 1)
                rows = slice(b * S, (b + 1) * S)
                split_low(k_lo[0:DC, rows], ps_b(b)[0:DC, 0:S], k_hi[0:DC, rows].bitcast(F32), klo_set)

            def queries_low(p, b):
                wait(v, qhi_set, 4 * p + b + 1)
                for h in range(2):
                    ins = nc.vector.tensor_tensor(q_hl[DC:P, b, h, :], ps_a[DC * h:DC * h + DC, 0:S],
                                                  q_hl[0:DC, b, h, :].bitcast(F32), ALU.subtract)
                ins.then_inc(qlo_set, 1)

            def maxima(p, b, h, nth):
                wait(v, s_done, 2 * (4 * p + b) + nth + 1)
                nc.vector.tensor_reduce(mx[:, b, 2 * h:2 * h + 2], ps_s[:, h, :].rearrange("p (c l) -> p c l", c=SC),
                                        AX_X, ALU.max).then_inc(max_set, 1)

            def context(p, b):
                g = 4 * p + b
                cs = ps_c[:, 0:4 * (DC + 1)].rearrange("p (n d) -> p n d", n=4)
                wait(v, pv_done, g + 1)
                nc.vector.reciprocal(rden[:, b, :], cs[:, :, DC]).then_inc(rec_set, 1)
                wait(v, rec_set, g + 1)
                nc.vector.tensor_tensor(cx[:, SC * b:SC * b + SC, p, :].rearrange("p c (h d) -> p h c d", h=2),
                                        cs[:, :, 0:DC].rearrange("p (h c) d -> p h c d", h=2),
                                        rden[:, b, :].rearrange("p (h c) -> p h c", h=2).unsqueeze(3)
                                        .broadcast_to([P, 2, SC, DC]), ALU.mult).then_inc(cx_set, 1)

            def context_low(t):
                v.wait_ge(cthi_set, t + 1)
                if t >= 2:
                    v.wait_ge(o_done, t - 1)
                nc.vector.tensor_tensor(ct_lo[:, t % 2].rearrange("p a b -> p (a b)"),
                                        ps_ct(t),
                                        ct_hi[:, t % 2].rearrange("p a b -> p (a b)").bitcast(F32),
                                        ALU.subtract).then_inc(ctlo_set, 1)

            moments(0)
            normalise(0)
            moments(1)
            normalise(1)
            turned_low(0)
            turned_low(1)
            fold_m(0)
            moments(2)
            keys_low(0)
            queries_low(0, 0)
            v.wait_ge(std_set, 3)
            last = slice(NT // 2, NT)
            link(nc.vector.reciprocal(rstd[:, last], std[:, last]))
            nc.vector.scalar_tensor_tensor(out=offset[:, last], in0=mv[:, last, 0], scalar=-1.0, in1=rstd[:, last],
                                           op0=ALU.mult, op1=ALU.mult).then_inc(offset_set, 1)
            keys_low(1)
            maxima(0, 0, 0, 0)
            queries_low(0, 1)
            maxima(0, 0, 1, 1)
            turned_low(2)
            v.wait_ge(v_done, 1)
            nc.vector.tensor_reduce(vmax[:], ps_c[:], AX_X, ALU.max,
                                    apply_absolute_value=True).then_inc(vmax_set, 1)
            turned_low(3)
            maxima(0, 1, 0, 0)
            maxima(0, 1, 1, 1)
            queries_low(0, 2)

            def values_scale():
                v.wait_ge(vall_set, 1)
                link(nc.vector.tensor_scalar(vinv[:], vall[:], TINY, 1.0 / V_TOP, ALU.max, ALU.mult))
                nc.vector.reciprocal(vscale[:], vinv[:]).then_inc(vinv_set, 1)

            def values_low():
                v.wait_ge(vhi_set, 1)
                nc.vector.scalar_tensor_tensor(out=v_lo[:], in0=ps_c[:].rearrange("p (t d) -> p t d", t=NT),
                                               scalar=vscale[:, 0:1], in1=v_hi[:, :, 0:DC],
                                               op0=ALU.mult, op1=ALU.subtract).then_inc(v_set, 1)
                v.wait_ge(tanh_set, 1)
                nc.vector.tensor_tensor(ga[:], tanhs[:, 0:1], vinv[:], ALU.mult)

            values_scale()
            keys_low(2)
            keys_low(3)

            def step(p):
                for b in range(B):
                    looks_2 = is_at_most(p, NP - 2) or b + 2 < B
                    looks_3 = is_at_most(p, NP - 2) or b + 3 < B
                    p2, b2 = p + (b + 2) // B, (b + 2) % B
                    folds_3 = b == 0 and is_at_most(p, NP - 2)
                    if looks_2 and not folds_3:
                        maxima(p2, b2, 1, 0)
                    if folds_3:
                        fold_m(p + 1)
                    if looks_3:
                        queries_low(p + (b + 3) // B, (b + 3) % B)
                    if looks_2:
                        maxima(p2, b2, 0, 0 if folds_3 else 1)
                    if looks_2 and folds_3:
                        maxima(p2, b2, 1, 1)
                    if b == 1:
                        fold_n(p)
                    if b >= 2:
                        context(p, b - 2)
                    elif not isinstance(p, int) or p > 0:
                        context(p - 1, b + 2)
                    if isinstance(p, int) and p == 0 and b == 0:
                        values_low()
                    if isinstance(p, int) and p == NP - 1 and b == 1:
                        v.wait_ge(whi_set, 1)
                        nc.vector.scalar_tensor_tensor(out=wffn_lo[:], in0=wffn[:], scalar=tanhs[:, 1:2],
                                                       in1=wffn_hi[:].bitcast(F32), op0=ALU.mult,
                                                       op1=ALU.subtract).then_inc(wlo_set, 1)
                    if isinstance(p, int) and p == NP - 1 and b == B - 2:
                        context_low(0)

            pairs(v, step)
            def normed_low(t):
                v.wait_ge(xt2hi_set, t + 1)
                nc.vector.tensor_tensor(xt2_lo[:, t % 2].rearrange("p c n -> p (c n)"), ps_x2,
                                        xt2_hi[:, t % 2].rearrange("p c n -> p (c n)").bitcast(F32),
                                        ALU.subtract).then_inc(xt2lo_set, 1)

            def residual(t):
                i = t % 2
                v.wait_ge(o_done, t + 1)
                if t >= 2:
                    v.wait_ge(x1b_set, t - 1)
                nc.vector.scalar_tensor_tensor(out=x1[:, i, :], in0=ps_o(t), scalar=ga[:, 0:1], in1=x_sb[:, t, :],
                                               op0=ALU.mult, op1=ALU.add).then_inc(x1_set, 1)
                v.wait_ge(x1_set, t + 1)
                nc.vector.bn_stats(st2[:, i, :], x1[:, i, :]).then_inc(st2_set, 1)
                if 1 <= t < NT - 1:
                    normed_low(t - 1)
                v.wait_ge(st2_set, t + 1)
                nc.vector.bn_aggr(mv2[:, i, :], st2[:, i, :]).then_inc(var2_set, 1)
                if t == NT - 1:
                    normed_low(t - 1)
                v.wait_ge(std2_set, t + 1)
                link(nc.vector.reciprocal(rs2[:, i:i + 1], sd2[:, i:i + 1]))
                nc.vector.tensor_scalar(xn2[:, i, :], x1[:, i, :], mv2[:, i, 0:1], rs2[:, i:i + 1],
                                        ALU.subtract, ALU.mult).then_inc(xn2_set, 1)

            def result(t):
                v.wait_ge(ffn_done, t + 1)
                v.wait_ge(x1b_set, t + 1)
                nc.vector.tensor_tensor(y[:, t, :], ps_y(t), x1b[:, t % 2, :], ALU.add).then_inc(y_set, 1)

            context_low(1)
            context(NP - 1, B - 2)
            for t in range(NT):
                residual(t)
                if t == 0:
                    context(NP - 1, B - 1)
                elif t < NT - 2:
                    result(t - 1)
                if t + 2 < NT:
                    context_low(t + 2)
            result(NT - 3)
            result(NT - 2)
            normed_low(NT - 1)
            result(NT - 1)

        @block.tensor
        def _(pe):
            def mm(o, lhsT, rhs, first, last):
                return nc.tensor.matmul(o, lhsT=lhsT, rhs=rhs, start=first, stop=last)

            def fold_1(p):
                wait(pe, f1w_in, 16 * (p + 1))
                kcq = f1w[:, 0:2 * 2 * K].rearrange("q (c h k) -> q c h k", c=2, h=2)
                wqr = f1w[:, 2 * 2 * K:].rearrange("q (c h r) -> q c h r", c=2, h=2)
                for h in range(2):
                    for c in range(2):
                        ins = mm(ps_f[:, R * h:R * h + R], kcq[:, c, h, :], wqr[:, c, h, :], c == 0, c == 1)
                ins.then_inc(f1_done, 1)

            def fold_2(p):
                wait(pe, g_set, p + 1)
                wait(pe, wq_in, 16 * (p + 1))
                for h in range(2):
                    ins = mm(ps_f[R * h:R * h + R, 0:DM], g_sb[:, R * h:R * h + R], wq[:, h, :], True, True)
                ins.then_inc(f2_done, 1)

            def fold_3(p):
                wait(pe, mtsb_set, p + 1)
                wait(pe, wkr_in, 16 * (p + 1))
                for c in range(IC):
                    ins = mm(ps_f[:, P * c:P * c + P], mt_sb[:, P * c:P * c + P], wkr[:], True, True)
                ins.then_inc(f3_done, 1)

            def fold_n(p):
                wait(pe, wo_in, 16 * (p + 1))
                for h in range(2):
                    ins = mm(ps_f[DC * h:DC * h + DC, 0:DM], wo[:, DC * h:DC * h + DC],
                             wo[:, 2 * DC + DM * h:2 * DC + DM * h + DM], True, True)
                ins.then_inc(nf_done, 1)

            def queries(p, b):
                wait(pe, mlo_set, p + 1)
                rows = slice(b * S, (b + 1) * S)
                n = 0
                for c in range(IC):
                    for w, xt in ((m_hi, xt_hi), (m_hi, xt_lo), (m_lo, xt_hi)):
                        ins = mm(ps_a[:, 0:S], w[:, c, :], xt[:, c, rows], n == 0, n == 3 * IC - 1)
                        n += 1
                ins.then_inc(q_done, 1)

            def scores(p, b, h):
                e = 4 * p + b
                wait(pe, qlo_set, e + 1)
                if h == 0:
                    wait(pe, mxt_set, e)
                else:
                    wait(pe, max_set, 2 * e)
                for c in range(SC):
                    ins = mm(ps_s[:, h, S * c:S * c + S], q_hl[:, b, h, P * c:P * c + P],
                             k_hi[:, b * S:(b + 1) * S], True, True)
                ins.then_inc(s_done, 1)

            def scores_t(p, b):
                g = 4 * p + b
                wait(pe, qhm_in[b], 16 * (p + 1))
                wait(pe, mrow_in[b], 16 * (p + 1))
                wait(pe, phi_set, g - 1)
                for j in range(SC):
                    keys = slice(b * S + P * j, b * S + P * j + P)
                    o = ps_t[:, b % 2, j, :]
                    mm(o, k_hi[:, keys], q_hl[:, b].rearrange("k h s -> k (h s)"), True, False)
                    ins = mm(o, k_lo[:, keys], q_hm[:, b].rearrange("k h s -> k (h s)"), False, True)
                ins.then_inc(st_done, 1)

            def turn_maxima(p, b):
                wait(pe, max_set, 2 * (4 * p + b) + 2)
                nc.tensor.transpose(ps_s[0:4, 0, 0:P], mx[:, b, :], ident).then_inc(mt_done, 1)

            def values(p, b):
                g = 4 * p + b
                wait(pe, plo_set, g + 1)
                wait(pe, cx_set, g)
                for h in range(2):
                    for c in range(SC):
                        at = (2 * h + c) * (DC + 1)
                        for j in range(SC):
                            ph = p_hi[:, b, j, h, P * c:P * c + P]
                            pl = p_lo[:, b, j, h, P * c:P * c + P]
                            vh, vl = v_hi[:, SC * b + j, :], v_lo[:, SC * b + j, :]
                            mm(ps_c[:, at:at + DC + 1], ph, vh, j == 0, False)
                            mm(ps_c[:, at:at + DC], ph, vl, False, False)
                            ins = mm(ps_c[:, at:at + DC + 1], pl, vh, False, j == SC - 1)
                ins.then_inc(pv_done, 1)

            def turn_context(t, first=0, end=NP):
                if t >= 2:
                    pe.wait_ge(ctlo_set, t - 1)
                if end == NP:
                    pe.wait_ge(cx_set, STEPS - B + t // SC + 1)
                for p in range(first, end):
                    ins = nc.tensor.transpose(ps_ct(t)[:, P * p:P * p + P], cx[:, t, p, :], ident)
                if end == NP:
                    ins.then_inc(ctt_done, 1)

            def turn_rows(b):
                for c in range(SC):
                    t = SC * b + c
                    if t < NT // 2:
                        pe.wait_ge(xn_set, t + 1)
                    else:
                        pe.wait_ge(xna_set, t - NT // 2 + 1)
                    for i in range(IC):
                        ins = nc.tensor.transpose(ps_b(b)[:, S * i + P * c:S * i + P * c + P],
                                                  xn[:, t, P * i:P * i + P], ident)
                ins.then_inc(xt_done, 1)

            def keys(b):
                pe.wait_ge(turned_set, b + 1)
                pe.wait_ge(xtlo_set, b + 1)
                mm(ps_b(b)[:, 0:S], ident4, turned[:, b * S:(b + 1) * S], True, True).then_inc(k_done, 1)

            fold_1(0)
            pe.wait_ge(ident_in, 16)
            turn_rows(0)
            fold_2(0)
            turn_rows(1)
            fold_3(0)
            keys(0)
            queries(0, 0)
            keys(1)
            fold_1(1)
            pe.wait_ge(qlo_set, 1)
            queries(0, 1)
            pe.wait_ge(klo_set, 1)
            scores(0, 0, 0)
            pe.wait_ge(g_set, 2)
            scores(0, 0, 1)
            turn_rows(2)
            pe.wait_ge(turned_set, B)
            for t in range(NT):
                ins = mm(ps_c[:, DC * t:DC * t + DC], turned[:, P * t:P * t + P], ident4[:, 0:DC], True, True)
            ins.then_inc(v_done, 1)
            turn_rows(3)
            pe.wait_ge(max_set, 2)
            fold_2(1)
            turn_maxima(0, 0)
            pe.wait_ge(qlo_set, 2)
            pe.wait_ge(xtlo_set, 3)
            queries(0, 2)
            pe.wait_ge(klo_set, 2)
            scores(0, 1, 0)
            pe.wait_ge(mtsb_set, 2)
            scores(0, 1, 1)
            keys(2)
            keys(3)

            def step(p):
                for b in range(B):
                    looks_1 = is_at_most(p, NP - 2) or b + 1 < B
                    looks_2 = is_at_most(p, NP - 2) or b + 2 < B
                    p1, b1 = p + (b + 1) // B, (b + 1) % B
                    p2, b2 = p + (b + 2) // B, (b + 2) % B
                    if looks_1 and rows_first(p, b):
                        turn_maxima(p1, b1)
                    if is_at_most(p, NP - 2) or b + 3 < B:
                        wait(pe, qlo_set, 4 * p + b + 3)
                        queries(p + (b + 3) // B, (b + 3) % B)
                    folds_3 = b == 0 and is_at_most(p, NP - 2)
                    if folds_3:
                        wait(pe, max_set, 2 * (4 * p + 2))
                        fold_3(p + 1)
                    if looks_1 and not rows_first(p, b):
                        turn_maxima(p1, b1)
                    if looks_2 and not folds_3:
                        if b == 2:
                            wait(pe, nlo_set, p + 1)
                        if b == 3 and is_at_most(p, NP - 3):
                            wait(pe, g_set, p + 3)
                        scores(p2, b2, 1)
                    if isinstance(p, int) and p == NP - 1 and b == B - 1:
                        pe.wait_ge(nlo_set, NP)
                        turn_context(0, 4, NP)
                    if isinstance(p, int) and p == 0 and b == 1:
                        pe.wait_ge(klo_set, B)
                    scores_t(p, b)
                    if looks_2:
                        scores(p2, b2, 0)
                    if folds_3:
                        wait(pe, mlo_set, p + 2)
                        scores(p2, b2, 1)
                    elif b == 1 or b > 1 and is_at_most(p, NP - 3):
                        wait(pe, max_set, 2 * (4 * p + b + 2) + 1)
                        (None, fold_n, fold_1, fold_2)[b](p if b == 1 else p + 2)
                    if isinstance(p, int) and p == 0 and b == 2:
                        pe.wait_ge(v_set, 1)
                    if b >= 2:
                        values(p, b - 2)
                    elif not isinstance(p, int) or p > 0:
                        values(p - 1, b + 2)
                    if isinstance(p, int) and p == NP - 1 and b == B - 2:
                        pe.wait_ge(mxt_set, STEPS)
                        turn_context(0, 0, 4)

            pairs(pe, step)
            def project(t):
                pe.wait_ge(ctlo_set, t + 1)
                if t == 2:
                    pe.wait_ge(cx_set, STEPS)
                if t >= 1:
                    pe.wait_ge(x1_set, max(1, t - 1))
                n = 0
                for p in range(NP):
                    for c, w in ((ct_hi, n_hi), (ct_hi, n_lo), (ct_lo, n_hi)):
                        ins = mm(ps_o(t), c[:, t % 2, p, :], w[:, p, :], n == 0, n == 3 * NP - 1)
                        n += 1
                ins.then_inc(o_done, 1)

            def linear(t):
                pe.wait_ge(xn2_set, t + 1)
                if t >= 1:
                    pe.wait_ge(xt2lo_set, t)
                for c in range(IC):
                    ins = nc.tensor.transpose(ps_x2[:, P * c:P * c + P], xn2[:, t % 2, P * c:P * c + P], ident)
                ins.then_inc(xt2_done, 1)

            def linear_mm(t):
                if t == 0:
                    pe.wait_ge(wlo_set, 1)
                elif t != NT - 2:
                    pe.wait_ge(y_set, min(t, NT - 2))
                n = 0
                for xt, w, ready in ((xt2_hi, wffn_hi, xt2hi_set), (xt2_hi, wffn_lo, xt2hi_set),
                                     (xt2_lo, wffn_hi, xt2lo_set)):
                    pe.wait_ge(ready, t + 1)
                    for c in range(IC):
                        ins = mm(ps_y(t), xt[:, t % 2, c, :], w[:, c, :], n == 0, n == 3 * IC - 1)
                        n += 1
                ins.then_inc(ffn_done, 1)

            pe.wait_ge(phi_set, STEPS - 1)
            turn_context(1)
            project(0)
            values(NP - 1, B - 2)
            turn_context(2)
            values(NP - 1, B - 1)
            project(1)
            for t in range(1, NT - 2):
                linear(t - 1)
                turn_context(t + 2)
                linear_mm(t - 1)
                project(t + 1)
            linear(NT - 3)
            project(NT - 1)
            linear(NT - 2)
            linear_mm(NT - 3)
            linear_mm(NT - 2)
            linear(NT - 1)
            linear_mm(NT - 1)


def _rope():
    import numpy as np
    inv = (1.0 / np.power(np.float32(10000.0), np.arange(0, DC, 2, dtype=np.float32) / np.float32(DC))).astype(np.float32)
    f = (np.arange(S, dtype=np.float32)[:, None] * inv[None, :]).astype(np.float32).astype(np.float64)
    sin, cos = np.repeat(np.sin(f), 2, -1), np.repeat(np.cos(f), 2, -1)
    sin[:, :DC // 2] *= -1.0
    return np.stack([cos, sin]).astype(np.float32)


def kernel(x, ctx_512, g_xattn, g_ffn, L0_xattn_Wq, L0_xattn_w_kc_q, L0_xattn_w_kc_kv, L0_xattn_W_qr,
           L0_xattn_W_kr, L0_xattn_Wo, L0_ffn_weight, L0_ffn_scale_weight, L0_ffn_bias):
    import numpy as np
    import concourse.bacc as bacc
    from concourse.bass_utils import run_bass_kernel_spmd

    A = lambda a: np.ascontiguousarray(np.asarray(a))
    kv = A(ctx_512)
    swapped = np.concatenate([kv[..., DC // 2:], kv[..., :DC // 2]], -1)
    both = np.stack([kv, swapped]).reshape(2, T, DC)
    rope = _rope()
    Wq, kcq, kckv = A(L0_xattn_Wq), A(L0_xattn_w_kc_q), A(L0_xattn_w_kc_kv)
    Wqr, Wkr, Wo = A(L0_xattn_W_qr), A(L0_xattn_W_kr), A(L0_xattn_Wo)
    kcq_t = kcq.reshape(NP, 2, K, 2, QC).transpose(0, 4, 3, 1, 2).reshape(NP, QC, 4 * K)
    wqr_t = Wqr.reshape(NP, 2, 2, QC, R).transpose(0, 3, 2, 1, 4).reshape(NP, QC, 4 * R)
    wkr_bd = np.zeros((NP, 2, R, 2, DC), np.float32)
    for h in range(2):
        wkr_bd[:, h, :, h, :] = Wkr.reshape(NP, 2, DC, R)[:, h].transpose(0, 2, 1)
    kckv_t = kckv.reshape(NP, 2, K, DC).transpose(0, 2, 1, 3).reshape(NP, K, 2 * DC)
    wo_t = Wo.T.reshape(NP, 2, K, DM).transpose(0, 2, 1, 3).reshape(NP, K, 2 * DM)
    arrays = {
        "x_rows": A(x).reshape(NT, P, DM),
        "kv_rope": np.concatenate([both.transpose(0, 2, 1), rope.transpose(0, 2, 1)], -1).reshape(P, T + S),
        "identities": np.stack([np.eye(P), np.tile(np.eye(DC), (2, 2))], 1).astype(np.float32),
        "w_f1": np.concatenate([kcq_t, wqr_t], -1),
        "w_q": Wq.reshape(NP, 2, K, DM).transpose(0, 2, 1, 3),
        "w_kr": wkr_bd.reshape(NP, P, P),
        "w_o": np.concatenate([kckv_t, wo_t], -1),
        "w_ffn": A(L0_ffn_weight).T.reshape(IC, P, DM).transpose(1, 0, 2),
        "rows_o": np.stack([A(L0_ffn_scale_weight), A(L0_ffn_bias)]),
        "gates": np.concatenate([A(g_xattn).reshape(1), A(g_ffn).reshape(1)]),
    }
    arrays = {f"{n}_dram": np.ascontiguousarray(a) for n, a in arrays.items()}
    nc = bacc.Bacc("TRN2", target_bir_lowering=False, num_devices=1)
    aps = [nc.dram_tensor(n, a.shape, mybir.dt.from_np(a.dtype), kind="ExternalInput").ap() for n, a in arrays.items()]
    aps[0] = aps[0].rearrange("t p n -> p t n")
    out = nc.dram_tensor("out_dram", (NT, P, DM), F32, kind="ExternalOutput").ap()
    flamingo_kernel(nc, *aps, out.rearrange("t p n -> p t n"))
    r = run_bass_kernel_spmd(nc, [arrays], core_ids=[0])
    return r.results[0]["out_dram"].reshape(B, S, DM)
```
